# Optimizing a Trainium2 kernel written in Bass

```python
import numpy as np
import jax
import jax.numpy as jnp

def _softmax(x, axis=-1):
    return jax.nn.softmax(x, axis=axis)

def _gelu(x):
    return jax.nn.gelu(x, approximate=True)

def _silu(x):
    return jax.nn.silu(x)

def _sigmoid(x):
    return jax.nn.sigmoid(x)

def _layernorm(x, axis=-1, eps=1e-05):
    m = jnp.mean(x, axis=axis, keepdims=True)
    v = jnp.var(x, axis=axis, keepdims=True)
    return (x - m) / jnp.sqrt(v + eps)

def _scatter_add(tgt, idx, src, axis=0):
    return tgt.at[idx].add(src)

def _segment_sum(src, seg, n):
    return jax.ops.segment_sum(src, seg, n)
kernel_name = 'mk_gnn_resnorm_d1_gnn_r8_656762'

def setup_inputs(seed: int=0):
    np.random.seed(seed)
    _w = jnp.asarray

    def _rec_inputs():
        import jax
        import jax.numpy as jnp
        _gk = jax.random.key(seed)
        x = -0.0005121 + 1.001 * jax.random.normal(jax.random.fold_in(_gk, 1), (12500, 32), jnp.float32)
        src = jax.random.randint(jax.random.fold_in(_gk, 2), (400000,), 0, 12500, jnp.int32)
        dst = jnp.minimum((12500 * jax.random.uniform(jax.random.fold_in(_gk, 3), (400000,)) ** 2.0).astype(jnp.int32), 99999)
        _o = jnp.argsort(dst, stable=True)
        src = src[_o]
        dst = dst[_o]
        edge_attr_32 = 0.000216709 + 1.00012 * jax.random.normal(jax.random.fold_in(_gk, 11), (400000, 32), jnp.float32)
        edge_attr_4 = 0.000714719 + 1.00021 * jax.random.normal(jax.random.fold_in(_gk, 12), (400000, 4), jnp.float32)
        return (x, src, dst, edge_attr_32, edge_attr_4)
    x, src, dst, edge_attr_32, edge_attr_4 = _rec_inputs()

    def _L0_gnn_setup():
        import jax, jax.numpy as jnp
        import numpy as np
        MUL = 8
        N_NODES = 12500
        N_EDGES = 100000
        EDGE_DIM = 32
        MLP_DIM = 64
        W_NUMEL = 4 * MUL * MUL
        ALPHA = 0.25
        C110 = 1.0 / np.sqrt(3.0)
        SI_SCALE = 1.0 / np.sqrt(MUL)
        key = jax.random.key(seed)
        ks = jax.random.split(key, 10)
        node_attr = jax.random.normal(ks[0], (N_NODES, 4 * MUL), dtype=jnp.float32)
        edge_index = jax.random.randint(ks[1], (2, N_EDGES), 0, N_NODES, dtype=jnp.int64)
        edge_sh = jax.random.normal(ks[2], (N_EDGES, 4), dtype=jnp.float32)
        edge_feat = jax.random.normal(ks[3], (N_EDGES, EDGE_DIM), dtype=jnp.float32)
        W1 = jax.random.normal(ks[4], (EDGE_DIM, MLP_DIM), dtype=jnp.float32) / np.sqrt(EDGE_DIM)
        b1 = jnp.zeros((MLP_DIM,), dtype=jnp.float32)
        W2 = jax.random.normal(ks[5], (MLP_DIM, W_NUMEL), dtype=jnp.float32) / np.sqrt(MLP_DIM)
        b2 = jnp.zeros((W_NUMEL,), dtype=jnp.float32)
        si_w0 = jax.random.normal(ks[6], (MUL, MUL), dtype=jnp.float32)
        si_w1 = jax.random.normal(ks[7], (MUL, MUL), dtype=jnp.float32)
        return {'node_attr': node_attr, 'edge_index': edge_index, 'edge_sh': edge_sh, 'edge_feat': edge_feat, 'W1': W1, 'b1': b1, 'W2': W2, 'b2': b2, 'si_w0': si_w0, 'si_w1': si_w1}
    _L0_gnn_all = _L0_gnn_setup()
    _L0_gnn_in = {k: v for k, v in _L0_gnn_all.items() if k in ('W1', 'b1', 'W2', 'b2', 'si_w0', 'si_w1')}
    del _L0_gnn_all
    return {'x': x, 'src': src, 'dst': dst, 'edge_attr_32': edge_attr_32, 'edge_attr_4': edge_attr_4, 'L0_gnn_W1': _L0_gnn_in['W1'], 'L0_gnn_b1': _L0_gnn_in['b1'], 'L0_gnn_W2': _L0_gnn_in['W2'], 'L0_gnn_b2': _L0_gnn_in['b2'], 'L0_gnn_si_w0': _L0_gnn_in['si_w0'], 'L0_gnn_si_w1': _L0_gnn_in['si_w1']}

def reference(x, src, dst, edge_attr_32, edge_attr_4, L0_gnn_W1, L0_gnn_b1, L0_gnn_W2, L0_gnn_b2, L0_gnn_si_w0, L0_gnn_si_w1):
    import jax
    import jax.numpy as jnp

    def _L0_gnn_ref(node_attr, edge_index, edge_sh, edge_feat, W1, b1, W2, b2, si_w0, si_w1):
        import jax, jax.numpy as jnp
        import numpy as np
        MUL = 8
        N_NODES = 12500
        N_EDGES = 100000
        EDGE_DIM = 32
        MLP_DIM = 64
        W_NUMEL = 4 * MUL * MUL
        ALPHA = 0.25
        C110 = 1.0 / np.sqrt(3.0)
        SI_SCALE = 1.0 / np.sqrt(MUL)
        n = node_attr.shape[0]
        e = edge_sh.shape[0]
        h = jax.nn.relu(edge_feat @ W1 + b1)
        w = (h @ W2 + b2).reshape(e, 4, MUL, MUL)
        w_000, w_011, w_101, w_110 = (w[:, 0], w[:, 1], w[:, 2], w[:, 3])
        s = node_attr[:, :MUL]
        v = node_attr[:, MUL:].reshape(n, MUL, 3)
        src, dst = (edge_index[0], edge_index[1])
        s_e = s[src]
        v_e = v[src]
        sh0 = edge_sh[:, 0]
        sh1 = edge_sh[:, 1:4]
        m0 = ALPHA * (jnp.einsum('ei,eio->eo', s_e * sh0[:, None], w_000) + C110 * jnp.einsum('eim,em,eio->eo', v_e, sh1, w_110))
        m1 = ALPHA * (jnp.einsum('ei,em,eio->eom', s_e, sh1, w_011) + jnp.einsum('eim,eio->eom', v_e * sh0[:, None, None], w_101))
        out0 = jax.ops.segment_sum(m0, dst, num_segments=n)
        out1 = jax.ops.segment_sum(m1.reshape(e, MUL * 3), dst, num_segments=n).reshape(n, MUL, 3)
        out0 = out0 + SI_SCALE * (s @ si_w0)
        out1 = out1 + SI_SCALE * jnp.einsum('nim,io->nom', v, si_w1)
        return jnp.concatenate([out0, out1.reshape(n, MUL * 3)], axis=-1)
    edge_index = jnp.stack([src, dst])
    x = _layernorm(x + _L0_gnn_ref(x, edge_index, edge_attr_4, edge_attr_32, L0_gnn_W1, L0_gnn_b1, L0_gnn_W2, L0_gnn_b2, L0_gnn_si_w0, L0_gnn_si_w1), axis=-1)
    return x

_drawn_inputs = setup_inputs


def setup_inputs(seed=0):
    import zlib

    import numpy as np

    out = dict(_drawn_inputs(seed))
    spreads = {'L0_gnn_b1': (0.0, 0.1), 'L0_gnn_b2': (0.0, 0.1)}
    factors = {}
    for name, (base, spread) in spreads.items():
        noise = np.random.default_rng([zlib.crc32(name.encode()), seed]).standard_normal(out[name].shape)
        drawn = base * np.exp(spread * noise) if base else spread * noise
        out[name] = jnp.asarray(drawn.astype(out[name].dtype))
    for name, factor in factors.items():
        out[name] = (out[name] * factor).astype(out[name].dtype)
    return out
```

```python
from contextlib import ExitStack

import concourse.bass as bass
from concourse import mybir

P = 128
F32 = mybir.dt.float32
I32 = mybir.dt.int32
ALU = mybir.AluOpType
ACT = mybir.ActivationFunctionType
AX_X = mybir.AxisListType.X

MUL = 8
TILES = 4
BATCH = TILES * P
UNROLL = 4
LOAD = 2
WINDOW = 64
HALF = MUL // 2 * MUL
NODE_J = 10
NODE_STEP = NODE_J * P
ALPHA = 0.25
EPS = 1e-5

W101, W000, W110, W011, W_ALL = 0, 64, 128, 192, 256
S_COL, ROW = 3 * MUL, 4 * MUL
B_COL = ROW
T_COL = 5 * HALF
MSG = T_COL + 3 * MUL
CHUNK_B = MSG - P
C_EYE, C_IOTA, C_FOLD_A, C_FOLD_B, C_ALL = 0, 128, 192, 224, 256


def at_least(eng, sem, value):
    if not isinstance(value, int) or value > 0:
        eng.wait_ge(sem, value)


def build(nc, x_rows, x_nodes, x_cols, src, dst, dst_first, dst_rows, feat, sh, w1, b1, w2,
          self_in_w, consts, out):
    n_nodes = out.shape[0]
    n_batches = dst_first.shape[1]
    n_iters = n_batches // UNROLL
    n_steps = x_nodes.shape[0] // NODE_STEP
    nodes_pad = n_steps * NODE_STEP
    assert n_batches % UNROLL == 0 and n_iters >= 3 and n_steps >= 2
    assert nodes_pad >= n_nodes + WINDOW
    last_rows = n_nodes - (n_steps - 1) * NODE_STEP
    assert last_rows % NODE_J == 0

    with ExitStack() as ctx:
        def sb(name, shape, dt=F32):
            return ctx.enter_context(nc.sbuf_tensor(name, shape, dt))

        def psum(name, shape):
            return ctx.enter_context(nc.psum_tensor(name, shape, F32))

        def sem(name):
            return ctx.enter_context(nc.semaphore(name))

        cst = sb("cst", [P, C_ALL])
        w1_sb = sb("w1_sb", [P, TILES, 64])
        b1_sb = sb("b1_sb", [64, 1])
        w2_sb = sb("w2_sb", [P, W_ALL])
        self_w = sb("self_w", [32, 32])
        self_ws = sb("self_ws", [32, 32])
        zero_row = sb("zero_row", [P, 1])
        one_col = sb("one_col", [P, 1])
        eps_col = sb("eps_col", [P, 1])
        dst_sb = sb("dst_sb", [P, n_batches * TILES], I32)
        first_sb = sb("first_sb", [P, n_batches], I32)
        neg_local = sb("neg_local", [P, n_batches * TILES])
        span = sb("span", [P, 4])
        worst = sb("worst", [1, 2])
        general = sb("general", [1, 1], I32)
        src_slot = [sb(f"src_slot{s}", [P, LOAD * TILES], I32) for s in range(2)]
        feat_slot = [sb(f"feat_slot{s}", [P, LOAD * P]) for s in range(2)]
        sh_slot = [sb(f"sh_slot{s}", [P, LOAD, TILES, 4]) for s in range(2)]
        rows = sb("rows", [P, UNROLL, TILES, ROW])
        hidden = [sb(f"hidden{s}", [P, BATCH]) for s in range(2)]
        inputs = [sb(f"inputs{s}", [P, TILES, ROW + MUL]) for s in range(2)]
        v_sh1 = sb("v_sh1", [P, TILES, 3, MUL])
        prod = sb("prod", [P, TILES, 5, MUL * MUL])
        prod_s = sb("prod_s", [P, TILES, MUL, MUL])
        sum_s = sb("sum_s", [P, TILES, MUL])
        msg = [sb(f"msg{s}", [P, TILES, MSG]) for s in range(2)]
        dist = sb("dist", [P, TILES, WINDOW])
        onehot = [sb(f"onehot{s}", [P, TILES, WINDOW]) for s in range(2)]
        acc = sb("acc", [P, 2, nodes_pad])
        stage = [sb(f"stage{s}", [P, 2, NODE_J, P]) for s in range(2)]
        xc_sb = [sb(f"xc_sb{s}", [32, NODE_STEP]) for s in range(2)]
        xn_sb = [sb(f"xn_sb{s}", [P, NODE_J, ROW]) for s in range(2)]
        res = sb("res", [P, NODE_J, ROW])
        cen = sb("cen", [P, NODE_J, ROW])
        sqr = sb("sqr", [P, NODE_J, ROW])
        mean = sb("mean", [P, 2, NODE_J])
        std = sb("std", [P, 3, NODE_J])
        y_sb = [sb(f"y_sb{s}", [P, NODE_J, ROW]) for s in range(2)]

        hid_ps = [psum(f"hid_ps{s}", [64, BATCH]) for s in range(2)]
        w_ps = [psum(f"w_ps{s}", [P, TILES, W_ALL]) for s in range(2)]
        win_ps = psum("win_ps", [P, 2, 512])

        consts_in = sem("consts_in")
        dst_in = sem("dst_in")
        self_in = sem("self_in")
        src_in = [sem(f"src_in{s}") for s in range(2)]
        feat_in = [sem(f"feat_in{s}") for s in range(2)]
        sh_in = [sem(f"sh_in{s}") for s in range(2)]
        gathered = [sem(f"gathered{u}") for u in range(UNROLL)]
        turn = sem("turn")
        zeroed = sem("zeroed")
        acc_zeroed = sem("acc_zeroed")
        checked = sem("checked")
        flag_ready = sem("flag_ready")
        viol_ready = sem("viol_ready")
        viol_row = sem("viol_row")
        hid_ready = sem("hid_ready")
        relu_done = sem("relu_done")
        w_ready = sem("w_ready")
        scaled = sem("scaled")
        dist_done = sem("dist_done")
        onehot_ready = sem("onehot_ready")
        v_sh1_done = sem("v_sh1_done")
        prod_v_done = sem("prod_v_done")
        b_done = sem("b_done")
        prod_s_done = sem("prod_s_done")
        prods_done = sem("prods_done")
        sum_s_done = sem("sum_s_done")
        halves_done = sem("halves_done")
        msg_ready = sem("msg_ready")
        scattered = sem("scattered")
        acc_done = sem("acc_done")
        added = sem("added")
        staged = sem("staged")
        nodes_in = [sem(f"nodes_in{s}") for s in range(2)]
        folded = sem("folded")
        norm = sem("norm")
        squared = sem("squared")
        rooted = sem("rooted")
        y_ready = sem("y_ready")
        y_out = [sem(f"y_out{s}") for s in range(2)]

        block = ctx.enter_context(nc.Block())

        def eye(n):
            return cst[:, C_EYE:C_EYE + n]

        iota = cst[:, C_IOTA:C_IOTA + WINDOW]

        def iterations(eng, step):
            step(0, True, False)
            with eng.Fori(1, n_iters - 1) as i:
                step(i, False, False)
            step(n_iters - 1, False, True)

        def node_steps(eng, step):
            with eng.Fori(0, n_steps - 3, 2) as k:
                step(k, 0, False)
                step(k + 1, 1, False)
            step(n_steps - 2, 0, False)
            step(n_steps - 1, 1, True)

        @block.sync
        def _(sp):
            def load_src(k, s):
                w = LOAD * TILES
                sp.dma_start(src_slot[s][:, :], src[:, bass.ds(k * w, w)]).then_inc(src_in[s], 16)

            def load_edges(k, s):
                w = LOAD * P
                sp.dma_start(feat_slot[s][:, :], feat[:, bass.ds(k * w, w)]).then_inc(feat_in[s], 16)
                w = LOAD * TILES * 4
                sp.dma_start(sh_slot[s][:, :, :, :].rearrange("p b t c -> p (b t c)"),
                             sh[:, bass.ds(k * w, w)]).then_inc(sh_in[s], 16)

            load_src(0, 0)
            load_src(1, 1)
            sp.dma_start(dst_sb[:, :], dst).then_inc(dst_in, 16)
            sp.dma_start(first_sb[:, :], dst_first.broadcast_to([P, n_batches])).then_inc(dst_in, 16)
            for to, what in ((cst[:, :], consts), (w1_sb[:, :, :].rearrange("p t k -> p (t k)"), w1),
                             (b1_sb[:, :], b1), (w2_sb[:, :], w2)):
                sp.dma_start(to, what).then_inc(consts_in, 16)
            load_edges(0, 0)
            sp.dma_start(self_w[:, :], self_in_w).then_inc(self_in, 16)

            def free_edges(n):
                at_least(sp, hid_ready, n)
                at_least(sp, msg_ready, n)

            def step(i):
                sp.wait_ge(gathered[0], 64 * i + 64)
                sp.wait_ge(gathered[1], 64 * i + 64)
                load_src(2 * i + 2, 0)
                free_edges(4 * i)
                load_edges(2 * i + 1, 1)
                sp.wait_ge(gathered[2], 64 * i + 64)
                sp.wait_ge(gathered[3], 64 * i + 64)
                load_src(2 * i + 3, 1)
                free_edges(4 * i + 2)
                load_edges(2 * i + 2, 0)

            step(0)
            with sp.Fori(1, n_iters - 1) as i:
                step(i)
            free_edges(n_batches - 4)
            load_edges(2 * n_iters - 1, 1)

            def nodes(k, s, last):
                if isinstance(k, int) and k < 2:
                    pass
                elif True:
                    sp.wait_ge(norm, 4 * k - 4)
                    sp.wait_ge(folded, k - 1)
                sp.dma_start(xc_sb[s][:, :], x_cols[:, bass.ds(k * NODE_STEP, NODE_STEP)]).then_inc(nodes_in[s], 16)
                sp.dma_start(xn_sb[s][:, :, :].rearrange("p j c -> p (j c)"),
                             x_nodes[bass.ds(k * NODE_STEP, NODE_STEP), :].rearrange("(p j) c -> p (j c)", p=P)
                             ).then_inc(nodes_in[s], 16)

            def results(k, s, last):
                sp.wait_ge(y_ready, k + 1)
                n = last_rows if last else NODE_STEP
                sp.dma_start(out[bass.ds(k * NODE_STEP, n), :].rearrange("(p j) c -> p (j c)", j=NODE_J),
                             y_sb[s][0:n // NODE_J, :, :].rearrange("p j c -> p (j c)")).then_inc(y_out[s], 16)

            nodes(0, 0, False)
            nodes(1, 1, False)
            with sp.Fori(0, n_steps - 3, 2) as k:
                results(k, 0, False)
                nodes(k + 2, 0, False)
                results(k + 1, 1, False)
                nodes(k + 3, 1, False)
            results(n_steps - 2, 0, False)
            results(n_steps - 1, 1, True)
            sp.wait_ge(y_out[0], 16 * (n_steps // 2))
            sp.wait_ge(y_out[1], 16 * (n_steps // 2))

        @block.gpsimd
        def _(pool):
            def step(i, first, last):
                for u in range(UNROLL):
                    at_least(pool, scaled, 4 * i + u - 3)
                    at_least(pool, prods_done, 4 * i + u - 3)
                    pool.wait_ge(src_in[u // LOAD], 16 * i + 16)
                    pool.sem_inc(turn, 1)
                    for t in range(TILES):
                        at = (u % LOAD) * TILES + t
                        pool.indirect_dma_start(
                            out=rows[:, u, t, :], out_offset=None, in_=x_rows,
                            in_offset=bass.IndirectOffsetOnAxis(ap=src_slot[u // LOAD][:, at:at + 1], axis=0),
                        ).then_inc(gathered[u], 16)

            iterations(pool, step)

        @block.tensor
        def _(pe):
            def hidden_layer(i, u):
                i, u = i + u // UNROLL, u % UNROLL
                slot = u // LOAD
                pe.wait_ge(feat_in[slot], 16 * i + 16)
                at_least(pe, relu_done, 4 * i + u - 1)
                at = (u % LOAD) * P
                for t in range(TILES):
                    mm = pe.matmul(hid_ps[u % 2][:, t * P:(t + 1) * P], w1_sb[:, t, :],
                                   feat_slot[slot][:, at:at + P], start=True, stop=True)
                mm.then_inc(hid_ready, 1)

            def edge_weights(i, u):
                i, u = i + u // UNROLL, u % UNROLL
                pe.wait_ge(relu_done, 4 * i + u + 1)
                at_least(pe, prods_done, 4 * i + u - 1)
                for t in range(TILES):
                    mm = pe.matmul(w_ps[u % 2][:, t, :], hidden[u % 2][:, t * P:(t + 1) * P],
                                   w2_sb[:, :], start=True, stop=True)
                mm.then_inc(w_ready, 1)

            def scatter(i, u, slow):
                m, hot = msg[u % 2], onehot[u % 2]
                pe.wait_ge(msg_ready, 4 * i + u + 1)
                if slow:
                    at_least(pe, acc_done, 4 * i + u)
                    for t in range(TILES):
                        to = win_ps[:, t // 2, (t % 2) * 256:(t % 2) * 256 + 256]
                        pe.matmul(to[:, 0:P], m[:, t, 0:P], eye(P), start=True, stop=True)
                        mm = pe.matmul(to[0:CHUNK_B, P:2 * P], m[:, t, P:MSG], eye(P), start=True, stop=True)
                    mm.then_inc(scattered, 1)
                    return
                pe.wait_ge(onehot_ready, 4 * i + u + 1)
                at_least(pe, acc_done, 4 * i + u - 1)
                for t in range(TILES):
                    pe.matmul(win_ps[:, u % 2, 0:WINDOW], m[:, t, 0:P], hot[:, t, :],
                              start=(t == 0), stop=(t == TILES - 1))
                for t in range(TILES):
                    mm = pe.matmul(win_ps[0:CHUNK_B, u % 2, WINDOW:2 * WINDOW], m[:, t, P:MSG], hot[:, t, :],
                                   start=(t == 0), stop=(t == TILES - 1))
                mm.then_inc(scattered, 1)

            def edges(slow):
                pe.wait_ge(consts_in, 16 * 4)
                pe.wait_ge(zeroed, 5)
                hidden_layer(0, 0)
                edge_weights(0, 0)
                hidden_layer(0, 1)

                def step(i, first, last):
                    for u in range(UNROLL):
                        if not last or u + 1 < UNROLL:
                            edge_weights(i, u + 1)
                        if not last or u + 2 < UNROLL:
                            hidden_layer(i, u + 2)
                        scatter(i, u, slow)

                iterations(pe, step)

            pe.wait_ge(consts_in, 16 * 4)
            pe.wait_ge(viol_ready, 1)
            pe.matmul(win_ps[0:1, 0, 0:P], span[:, 3:4], eye(P), start=True, stop=True).then_inc(viol_row, 1)
            pe.wait_ge(flag_ready, 1)
            flag = pe.value_load(general[0:1, 0:1], min_val=0, max_val=1)
            with pe.If(flag == 0):
                edges(False)
            with pe.Else():
                edges(True)

            def fold(k, s, last):
                pe.wait_ge(staged, k + 1)
                pe.wait_ge(nodes_in[s], 16 * (k - s) + 32)
                if not (isinstance(k, int) and k < 2):
                    pe.wait_ge(norm, 4 * k - 7)
                for j in range(NODE_J):
                    to = hid_fold[s][:, j, :]
                    pe.matmul(to, stage[s][:, 0, j, :], cst[:, C_FOLD_A:C_FOLD_A + ROW], start=True, stop=False)
                    pe.matmul(to, stage[s][0:CHUNK_B, 1, j, :], cst[0:CHUNK_B, C_FOLD_B:C_FOLD_B + ROW],
                              start=False, stop=False)
                    mm = pe.matmul(to, xc_sb[s][:, j:NODE_STEP:NODE_J], self_ws[:, :], start=False, stop=True)
                mm.then_inc(folded, 1)

            hid_fold = [w_ps[s][:, 0:2, :].rearrange("p t c -> p (t c)")[:, 0:NODE_J * ROW]
                        .rearrange("p (j c) -> p j c", c=ROW) for s in range(2)]
            pe.wait_ge(checked, 6)
            fold(0, 0, False)
            fold(1, 1, False)
            with pe.Fori(2, n_steps - 1, 2) as k:
                fold(k, 0, False)
                fold(k + 1, 1, False)

        @block.scalar
        def _(act):
            act.wait_ge(zeroed, 1)
            act.activation(acc[:, 1, :], zero_row[:, 0:1].broadcast_to([P, nodes_pad]), ACT.Copy).then_inc(acc_zeroed, 1)

            def relu(i, u):
                i, u = i + u // UNROLL, u % UNROLL
                act.wait_ge(hid_ready, 4 * i + u + 1)
                at_least(act, w_ready, 4 * i + u - 1)
                act.activation(hidden[u % 2][0:64, :], hid_ps[u % 2][:, :], ACT.Relu,
                               bias=b1_sb[:, 0:1]).then_inc(relu_done, 1)

            def scale_rows(i, u):
                i, u = i + u // UNROLL, u % UNROLL
                act.wait_ge(gathered[u], 64 * i + 64)
                if u % LOAD == 0:
                    act.wait_ge(sh_in[u // LOAD], 16 * i + 16)
                at_least(act, prods_done, 4 * i + u - 1)
                for t in range(TILES):
                    op = act.activation(inputs[u % 2][:, t, 0:ROW], rows[:, u, t, :], ACT.Copy,
                                        scale=sh_slot[u // LOAD][:, u % LOAD, t, 0:1])
                op.then_inc(scaled, 1)

            def distances(i, u):
                at_least(act, onehot_ready, 4 * i + u)
                for t in range(TILES):
                    op = act.activation(dist[:, t, :], iota, ACT.Abs,
                                        bias=neg_local[:, bass.ds((4 * i + u) * TILES + t, 1)])
                op.then_inc(dist_done, 1)

            def one_hot(i, u):
                act.wait_ge(dist_done, 4 * i + u + 1)
                at_least(act, scattered, 4 * i + u - 1)
                act.activation(onehot[u % 2][:, :, :], dist[:, :, :], ACT.Relu,
                               bias=one_col[:, 0:1], scale=-1.0).then_inc(onehot_ready, 1)

            def edges(slow):
                act.wait_ge(consts_in, 16 * 4)
                relu(0, 0)
                scale_rows(0, 0)

                def step(i, first, last):
                    for u in range(UNROLL):
                        more = not last or u + 1 < UNROLL
                        if more:
                            relu(i, u + 1)
                        if not slow:
                            distances(i, u)
                        if more:
                            scale_rows(i, u + 1)
                        if not slow:
                            one_hot(i, u)

                iterations(act, step)

            act.wait_ge(flag_ready, 1)
            flag = act.value_load(general[0:1, 0:1], min_val=0, max_val=1)
            with act.If(flag == 0):
                edges(False)
            with act.Else():
                edges(True)

            def stage_nodes(k, s, last):
                if not (isinstance(k, int) and k < 2):
                    act.wait_ge(folded, k - 1)
                act.activation(stage[s][:, :, :, :],
                               acc[:, :, bass.ds(k * NODE_STEP, NODE_STEP)].rearrange("p c (n j) -> p c j n", j=NODE_J),
                               ACT.Copy).then_inc(staged, 1)

            def layer_norm(k, s, last):
                act.wait_ge(norm, 4 * k + 3)
                act.activation(sqr[:, :, :], cen[:, :, :], ACT.Square).then_inc(squared, 1)
                act.wait_ge(norm, 4 * k + 4)
                act.activation(std[:, 1, :], std[:, 0, :], ACT.Sqrt, bias=eps_col[:, 0:1],
                               scale=1.0 / ROW).then_inc(rooted, 1)

            act.wait_ge(acc_done, n_batches)
            stage_nodes(0, 0, False)
            stage_nodes(1, 1, False)
            with act.Fori(0, n_steps - 3, 2) as k:
                layer_norm(k, 0, False)
                stage_nodes(k + 2, 0, False)
                layer_norm(k + 1, 1, False)
                stage_nodes(k + 3, 1, False)
            layer_norm(n_steps - 2, 0, False)
            layer_norm(n_steps - 1, 1, True)

        @block.vector
        def _(dve):
            dve.memset(zero_row[:, :], 0.0).then_inc(zeroed, 1)
            for s in range(2):
                dve.memset(hidden[s][64:P, :], 0.0).then_inc(zeroed, 1)
            dve.wait_ge(zeroed, 3)
            for s in range(2):
                dve.memset(hidden[s][64:65, :], 1.0).then_inc(zeroed, 1)
            dve.memset(one_col[:, :], 1.0).then_inc(zeroed, 1)
            dve.memset(eps_col[:, :], EPS).then_inc(zeroed, 1)
            dve.memset(acc[:, 0, :], 0.0).then_inc(zeroed, 1)
            for b in range(2):
                dve.memset(win_ps[:, b, :], 0.0).then_inc(zeroed, 1)

            dve.wait_ge(dst_in, 32)
            dve.tensor_tensor(neg_local[:, :].rearrange("p (b t) -> p b t", t=TILES),
                              first_sb[:, :].unsqueeze(2).broadcast_to([P, n_batches, TILES]),
                              dst_sb[:, :].rearrange("p (b t) -> p b t", t=TILES),
                              ALU.subtract).then_inc(checked, 1)
            dve.wait_ge(checked, 1)
            dve.tensor_reduce(span[:, 0:1], neg_local[:, :], AX_X, ALU.max).then_inc(checked, 1)
            dve.tensor_reduce(span[:, 1:2], neg_local[:, :], AX_X, ALU.min).then_inc(checked, 1)
            dve.wait_ge(checked, 3)
            dve.tensor_scalar(span[:, 2:3], span[:, 1:2], -1.0, float(1 - WINDOW), ALU.mult, ALU.add).then_inc(checked, 1)
            dve.wait_ge(checked, 4)
            dve.wait_ge(zeroed, 10)
            dve.tensor_tensor(span[:, 3:4], span[:, 0:1], span[:, 2:3], ALU.max).then_inc(viol_ready, 1)
            dve.wait_ge(viol_row, 1)
            dve.tensor_reduce(worst[:, 0:1], win_ps[0:1, 0, 0:P], AX_X, ALU.max).then_inc(checked, 1)
            dve.wait_ge(checked, 5)
            dve.tensor_scalar(general[:, :], worst[:, 0:1], 0.0, None, ALU.is_gt).then_inc(flag_ready, 1)
            dve.wait_ge(self_in, 16)
            dve.tensor_scalar(self_ws[:, :], self_w[:, :], float(MUL) ** -0.5, None, ALU.mult).then_inc(checked, 1)

            def messages(i, u):
                g = 4 * i + u
                shv = sh_slot[u // LOAD][:, u % LOAD, :, :]
                r, y, w, m = rows[:, u, :, :], inputs[u % 2], w_ps[u % 2], msg[u % 2]
                at_least(dve, msg_ready, g)
                dve.wait_ge(gathered[u], 64 * i + 64)
                if u % LOAD == 0:
                    dve.wait_ge(sh_in[u // LOAD], 16 * i + 16)
                dve.tensor_tensor(v_sh1[:, :, :, :], r[:, :, 0:S_COL].rearrange("p t (m i) -> p t m i", m=3),
                                  shv[:, :, 1:4].unsqueeze(3).broadcast_to([P, TILES, 3, MUL]),
                                  ALU.mult).then_inc(v_sh1_done, 1)
                dve.wait_ge(w_ready, g + 1)
                dve.tensor_tensor(prod_s[:, :, :, :],
                                  w[:, :, W011:W_ALL].rearrange("p t (i o) -> p t i o", o=MUL),
                                  r[:, :, S_COL:ROW].unsqueeze(3).broadcast_to([P, TILES, MUL, MUL]),
                                  ALU.mult).then_inc(prod_s_done, 1)
                dve.wait_ge(v_sh1_done, g + 1)
                dve.tensor_reduce(y[:, :, B_COL:B_COL + MUL], v_sh1[:, :, :, :].rearrange("p t m i -> p t i m"),
                                  AX_X, ALU.add).then_inc(b_done, 1)
                dve.wait_ge(scaled, g + 1)
                dve.tensor_tensor(
                    prod[:, :, 0:3, :].rearrange("p t m (i o) -> p t m i o", o=MUL),
                    w[:, :, W101:W000].rearrange("p t (i o) -> p t i o", o=MUL).unsqueeze(2)
                    .broadcast_to([P, TILES, 3, MUL, MUL]),
                    y[:, :, 0:S_COL].rearrange("p t (m i) -> p t m i", m=3).unsqueeze(4)
                    .broadcast_to([P, TILES, 3, MUL, MUL]), ALU.mult).then_inc(prod_v_done, 1)
                dve.wait_ge(b_done, g + 1)
                dve.tensor_tensor(
                    prod[:, :, 3:5, :].rearrange("p t b (i o) -> p t (b i) o", o=MUL),
                    w[:, :, W000:W011].rearrange("p t (i o) -> p t i o", o=MUL),
                    y[:, :, S_COL:ROW + MUL].unsqueeze(3).broadcast_to([P, TILES, 2 * MUL, MUL]),
                    ALU.mult).then_inc(prods_done, 1)
                dve.wait_ge(prod_s_done, g + 1)
                dve.tensor_reduce(sum_s[:, :, :], prod_s[:, :, :, :].rearrange("p t i o -> p t o i"),
                                  AX_X, ALU.add).then_inc(sum_s_done, 1)
                dve.wait_ge(prod_v_done, g + 1)
                dve.wait_ge(prods_done, g + 1)
                at_least(dve, scattered, g - 1)
                dve.tensor_tensor(m[:, :, 0:T_COL].rearrange("p t (b c) -> p t b c", c=HALF),
                                  prod[:, :, :, 0:HALF], prod[:, :, :, HALF:2 * HALF],
                                  ALU.add).then_inc(halves_done, 1)
                dve.wait_ge(sum_s_done, g + 1)
                dve.tensor_tensor(m[:, :, T_COL:MSG].rearrange("p t (m o) -> p t m o", m=3),
                                  sum_s[:, :, :].unsqueeze(2).broadcast_to([P, TILES, 3, MUL]),
                                  shv[:, :, 1:4].unsqueeze(3).broadcast_to([P, TILES, 3, MUL]),
                                  ALU.mult).then_inc(msg_ready, 1)

            def accumulate(i, u, slow):
                g = 4 * i + u
                if slow:
                    n = g + 1 if isinstance(g, int) else dve.snap(g + 1)
                    dve.wait_ge(flag_ready, 1)
                    dve.wait_ge(scattered, n)
                    for t in range(TILES):
                        col = (t % 2) * 256
                        with dve.Fori(0, P) as e:
                            node = dve.value_load(dst_rows[:, bass.ds(g * BATCH + t * P + e, 1)],
                                                  min_val=0, max_val=n_nodes - 1)
                            to = acc[:, :, bass.ds(node, 1)]
                            column = win_ps[:, t // 2, bass.ds(e + col, P + 1)][:, 0:P + 1:P].unsqueeze(2)
                            dve.tensor_tensor(to, to, column, ALU.add)
                            dve.drain()
                    dve.sem_inc(acc_done, 1)
                    return
                node = dve.value_load(first_sb[0:1, bass.ds(g, 1)], min_val=0, max_val=n_nodes - 1)
                at_least(dve, acc_done, g)
                dve.wait_ge(scattered, g + 1)
                to = acc[:, :, bass.ds(node, WINDOW)]
                dve.tensor_tensor(to, to, win_ps[:, u % 2, 0:2 * WINDOW].rearrange("p (c n) -> p c n", c=2),
                                  ALU.add).then_inc(acc_done, 1)

            def edges(slow):
                dve.wait_ge(acc_zeroed, 1)

                def step(i, first, last):
                    for u in range(UNROLL):
                        messages(i, u)
                        if not first or u > 0:
                            accumulate(i, u - 1, slow)

                iterations(dve, step)
                accumulate(n_iters - 1, UNROLL - 1, slow)

            dve.wait_ge(flag_ready, 1)
            flag = dve.value_load(general[0:1, 0:1], min_val=0, max_val=1)
            with dve.If(flag == 0):
                edges(False)
            with dve.Else():
                edges(True)

            def layer_norm(k, s, last):
                ps = w_ps[s][:, 0:2, :].rearrange("p t c -> p (t c)")[:, 0:NODE_J * ROW].rearrange("p (j c) -> p j c", c=ROW)
                dve.wait_ge(nodes_in[s], 16 * (k - s) + 32)
                dve.wait_ge(folded, k + 1)
                dve.tensor_tensor(res[:, :, :], ps, xn_sb[s][:, :, :], ALU.add).then_inc(norm, 1)
                dve.wait_ge(norm, 4 * k + 1)
                dve.tensor_reduce(mean[:, 0, :], res[:, :, :], AX_X, ALU.add).then_inc(norm, 1)
                dve.wait_ge(norm, 4 * k + 2)
                dve.scalar_tensor_tensor(out=cen[:, :, :], in0=mean[:, 0, :].unsqueeze(2).broadcast_to([P, NODE_J, ROW]),
                                         scalar=-1.0 / ROW, in1=res[:, :, :], op0=ALU.mult,
                                         op1=ALU.add).then_inc(norm, 1)
                dve.wait_ge(squared, k + 1)
                dve.tensor_reduce(std[:, 0, :], sqr[:, :, :], AX_X, ALU.add).then_inc(norm, 1)
                dve.wait_ge(rooted, k + 1)
                dve.reciprocal(std[:, 2, :], std[:, 1, :]).then_inc(checked, 1)
                dve.wait_ge(checked, k + 7)
                if not (isinstance(k, int) and k < 2):
                    dve.wait_ge(y_out[s], 8 * (k - s))
                dve.tensor_tensor(y_sb[s][:, :, :], cen[:, :, :],
                                  std[:, 2, :].unsqueeze(2).broadcast_to([P, NODE_J, ROW]),
                                  ALU.mult).then_inc(y_ready, 1)

            layer_norm(0, 0, False)
            layer_norm(1, 1, False)
            with dve.Fori(2, n_steps - 1, 2) as k:
                layer_norm(k, 0, False)
                layer_norm(k + 1, 1, False)


def constants():
    import numpy as np

    c = np.zeros((P, C_ALL), np.float32)
    c[:, C_EYE:C_EYE + P] = np.eye(P, dtype=np.float32)
    c[:, C_IOTA:C_IOTA + WINDOW] = np.arange(WINDOW, dtype=np.float32)
    c110 = 1.0 / np.sqrt(3.0)
    for o in range(MUL):
        for part in range(MUL // 2):
            for m in range(3):
                c[m * HALF + part * MUL + o, C_FOLD_A + MUL + 3 * o + m] = ALPHA
            c[3 * HALF + part * MUL + o, C_FOLD_A + o] = ALPHA
            c[part * MUL + o, C_FOLD_B + o] = ALPHA * c110
        for m in range(3):
            c[HALF + m * MUL + o, C_FOLD_B + MUL + 3 * o + m] = ALPHA
    return c


def layouts(x, src, dst, edge_attr_32, edge_attr_4, L0_gnn_W1, L0_gnn_b1, L0_gnn_W2, L0_gnn_b2,
            L0_gnn_si_w0, L0_gnn_si_w1):
    import numpy as np

    x, src, dst, feat, sh = (np.asarray(a) for a in (x, src, dst, edge_attr_32, edge_attr_4))
    n, e = x.shape[0], src.shape[0]
    per = BATCH * UNROLL
    pad = -e % per
    batches = (e + pad) // BATCH
    steps = -(-(n + WINDOW) // NODE_STEP)
    steps += steps % 2
    src = np.pad(src, (0, pad), mode="edge")
    dst = np.pad(dst, (0, pad), mode="edge")
    feat = np.pad(feat, ((0, pad), (0, 0)))
    sh = np.pad(sh, ((0, pad), (0, 0)))
    x_rows = np.concatenate([x[:, 8:].reshape(n, 8, 3).transpose(0, 2, 1).reshape(n, 24), x[:, :8]], axis=1)
    more = steps * NODE_STEP - n
    w2 = np.asarray(L0_gnn_W2).reshape(64, 4, 64)[:, [2, 0, 3, 1]].reshape(64, 256)
    b2 = np.asarray(L0_gnn_b2).reshape(1, 4, 64)[:, [2, 0, 3, 1]].reshape(1, 256)
    w1 = np.zeros((TILES, 32, TILES, 64), x.dtype)
    for t in range(TILES):
        w1[t, :, t] = np.asarray(L0_gnn_W1)
    w2 = np.pad(np.concatenate([w2, b2]), ((0, P - 65), (0, 0)))
    self_w = np.zeros((32, 32), x.dtype)
    self_w[24:, :8] = np.asarray(L0_gnn_si_w0)
    for m in range(3):
        self_w[8 * m:8 * m + 8, 8 + m::3] = np.asarray(L0_gnn_si_w1)
    return {
        "x_rows": x_rows,
        "x_nodes": np.pad(x, ((0, more), (0, 0))),
        "x_cols": np.pad(x_rows, ((0, more), (0, 0))).T,
        "src": src.reshape(batches * TILES, P).T,
        "dst": dst.reshape(batches * TILES, P).T,
        "dst_first": dst[::BATCH].reshape(1, batches),
        "dst_rows": dst.reshape(1, -1),
        "feat": feat.reshape(batches, TILES, P, 32).transpose(1, 3, 0, 2).reshape(P, -1),
        "sh": sh.reshape(batches * TILES, P, 4).transpose(1, 0, 2).reshape(P, -1),
        "w1": w1.reshape(P, -1),
        "b1": np.asarray(L0_gnn_b1).reshape(64, 1),
        "w2": w2,
        "self_in_w": self_w,
        "consts": constants(),
    }


def kernel(**inputs):
    import numpy as np
    import concourse.bacc as bacc
    from concourse.bass_utils import run_bass_kernel_spmd

    nc = bacc.Bacc("TRN2", target_bir_lowering=False, num_devices=1)
    arrays = {k: np.ascontiguousarray(a) for k, a in layouts(**inputs).items()}
    args = {k: nc.dram_tensor(f"{k}_dram", a.shape, mybir.dt.from_np(a.dtype), kind="ExternalInput").ap()
            for k, a in arrays.items()}
    out = nc.dram_tensor("out_dram", inputs["x"].shape, F32, kind="ExternalOutput").ap()
    build(nc, out=out, **args)
    r = run_bass_kernel_spmd(nc, [{f"{k}_dram": a for k, a in arrays.items()}], core_ids=[0])
    return r.results[0]["out_dram"]
```

```python
from contextlib import ExitStack

import concourse.bass as bass
from concourse import mybir

P = 128
F32 = mybir.dt.float32
I32 = mybir.dt.int32
ALU = mybir.AluOpType
ACT = mybir.ActivationFunctionType
AX_X = mybir.AxisListType.X

MUL = 8
TILES = 4
BATCH = TILES * P
UNROLL = 4
LOAD = 2
WINDOW = 64
HALF = MUL // 2 * MUL
QUARTERS = 4
NODE_P, NODE_J = 100, 4
NODE_STEP = NODE_P * NODE_J
GROUPS = QUARTERS * NODE_J
SELF_ROW = 64
ALPHA = 0.25
EPS = 1e-5

W101, W000, W110, W011, W_ALL = 0, 64, 128, 192, 256
S_COL, ROW = 3 * MUL, 4 * MUL
B_COL = ROW
T_COL = 5 * HALF
MSG = T_COL + 3 * MUL
CHUNK_B = MSG - P
C_EYE, C_IOTA, C_FOLD, C_ALL = 0, 128, (192, 224), 256


def at_least(eng, sem, value):
    if not isinstance(value, int) or value > 0:
        eng.wait_ge(sem, value)


def build(nc, x_rows, x_cols, src, dst, dst_first, dst_rows, feat, sh, w1, b1, w2,
          self_in_w, consts, out, n_tiles):
    n_nodes = out.shape[0]
    n_batches = -(-n_tiles // TILES)
    padded = dst_first.shape[1]
    n_iters = -(-n_batches // UNROLL)
    tail = n_batches - UNROLL * (n_iters - 1)
    tail_tiles = n_tiles - TILES * (n_batches - 1)
    nodes_pad = x_cols.shape[1]
    quarter = nodes_pad // QUARTERS
    n_steps = quarter // NODE_STEP
    assert n_iters >= 4 and n_steps >= 2 and tail >= 2
    assert nodes_pad == QUARTERS * n_steps * NODE_STEP >= n_nodes + WINDOW

    with ExitStack() as ctx:
        def sb(name, shape, dt=F32):
            return ctx.enter_context(nc.sbuf_tensor(name, shape, dt))

        def psum(name, shape):
            return ctx.enter_context(nc.psum_tensor(name, shape, F32))

        def sem(name):
            return ctx.enter_context(nc.semaphore(name))

        cst = sb("cst", [P, C_ALL])
        w1_sb = sb("w1_sb", [P, TILES, 64])
        b1_sb = sb("b1_sb", [P, 1])
        w2_sb = sb("w2_sb", [P, W_ALL])
        zero_row = sb("zero_row", [P, 1])
        one_col = sb("one_col", [P, 1])
        eps_col = sb("eps_col", [P, 1])
        dst_sb = sb("dst_sb", [P, padded * TILES], I32)
        first_sb = sb("first_sb", [P, padded], I32)
        neg_local = sb("neg_local", [P, padded * TILES])
        span = sb("span", [P, 4])
        worst = sb("worst", [1, 2])
        general = sb("general", [1, 1], I32)
        src_slot = [sb(f"src_slot{s}", [P, LOAD * TILES], I32) for s in range(2)]
        feat_slot = [sb(f"feat_slot{s}", [P, LOAD * P]) for s in range(2)]
        sh_slot = [sb(f"sh_slot{s}", [P, LOAD, TILES, 4]) for s in range(2)]
        rows = sb("rows", [P, UNROLL, TILES, ROW])
        hidden = [sb(f"hidden{s}", [P, BATCH]) for s in range(2)]
        inputs = [sb(f"inputs{s}", [P, TILES, ROW + MUL]) for s in range(2)]
        v_sh1 = sb("v_sh1", [P, TILES, 3, MUL])
        prod = sb("prod", [P, TILES, 5, MUL * MUL])
        prod_s = sb("prod_s", [P, TILES, MUL, MUL])
        sum_s = sb("sum_s", [P, TILES, MUL])
        msg = [sb(f"msg{s}", [P, TILES, MSG]) for s in range(2)]
        dist = sb("dist", [P, TILES, WINDOW])
        onehot = [sb(f"onehot{s}", [P, TILES, WINDOW]) for s in range(2)]
        acc = sb("acc", [P, 2, nodes_pad])
        by_column = [sb(f"by_column{s}", [P, NODE_STEP]) for s in range(2)]
        total = sb("total", [P, n_steps, GROUPS])
        centred = sb("centred", [P, n_steps, GROUPS, ROW])
        squares = [sb(f"squares{s}", [P, GROUPS, ROW]) for s in range(2)]
        spread = sb("spread", [P, 3, n_steps, GROUPS])
        y_sb = sb("y_sb", [P, QUARTERS, n_steps, NODE_J, ROW])

        hid_ps = [psum(f"hid_ps{s}", [P, 2, P]) for s in range(2)]
        w_ps = [psum(f"w_ps{s}", [P, TILES, W_ALL]) for s in range(2)]
        win_ps = psum("win_ps", [P, 2, 512])

        consts_in = sem("consts_in")
        dst_in = sem("dst_in")
        src_in = [sem(f"src_in{s}") for s in range(2)]
        feat_in = [sem(f"feat_in{s}") for s in range(2)]
        sh_in = [sem(f"sh_in{s}") for s in range(2)]
        gathered = [sem(f"gathered{u}") for u in range(UNROLL)]
        turn = sem("turn")
        zeroed = sem("zeroed")
        acc_zeroed = sem("acc_zeroed")
        checked = sem("checked")
        flag_ready = sem("flag_ready")
        viol_ready = sem("viol_ready")
        viol_row = sem("viol_row")
        hid_ready = sem("hid_ready")
        relu_done = sem("relu_done")
        w_ready = sem("w_ready")
        scaled = sem("scaled")
        dist_done = sem("dist_done")
        onehot_ready = sem("onehot_ready")
        v_sh1_done = sem("v_sh1_done")
        prod_v_done = sem("prod_v_done")
        b_done = sem("b_done")
        prod_s_done = sem("prod_s_done")
        prods_done = sem("prods_done")
        sum_s_done = sem("sum_s_done")
        halves_done = sem("halves_done")
        msg_ready = sem("msg_ready")
        scattered = sem("scattered")
        acc_done = sem("acc_done")
        added = sem("added")
        acc_copied = sem("acc_copied")
        x_in = sem("x_in")
        folded = sem("folded")
        fold_read = sem("fold_read")
        turned = sem("turned")
        totals = sem("totals")
        centres = sem("centres")
        squared = sem("squared")
        squares_summed = sem("squares_summed")
        rooted = sem("rooted")
        inverted = sem("inverted")
        y_ready = sem("y_ready")
        y_out = sem("y_out")

        block = ctx.enter_context(nc.Block())

        def eye(n):
            return cst[:, C_EYE:C_EYE + n]

        iota = cst[:, C_IOTA:C_IOTA + WINDOW]

        def iterations(eng, step):
            step(0, True, False)
            with eng.Fori(1, n_iters - 1) as i:
                step(i, False, False)
            step(n_iters - 1, False, True)

        def batches(last):
            return tail if last else UNROLL

        def rows_there(i, u, last):
            return 64 * i + 16 * (tail_tiles if last and u == tail - 1 else TILES)

        fold_ps = [w_ps[s][:, 0:2, :].rearrange("p t c -> p (t c)")[:, 0:NODE_STEP] for s in range(2)]
        node_ps = [w_ps[s][:, 2:4, :].rearrange("p t c -> p (t c)") for s in range(2)]

        @block.sync
        def _(sp):
            def load_src(k, s):
                w = LOAD * TILES
                sp.dma_start(src_slot[s][:, :], src[:, bass.ds(k * w, w)]).then_inc(src_in[s], 16)

            def load_edges(k, s):
                w = LOAD * P
                sp.dma_start(feat_slot[s][:, :], feat[:, bass.ds(k * w, w)]).then_inc(feat_in[s], 16)
                w = LOAD * TILES * 4
                sp.dma_start(sh_slot[s][:, :, :, :].rearrange("p b t c -> p (b t c)"),
                             sh[:, bass.ds(k * w, w)]).then_inc(sh_in[s], 16)

            load_src(0, 0)
            load_src(1, 1)
            sp.dma_start(dst_sb[:, :], dst).then_inc(dst_in, 16)
            sp.dma_start(first_sb[:, :], dst_first.broadcast_to([P, padded])).then_inc(dst_in, 16)
            for to, what in ((cst[:, 0:C_FOLD[1]], consts[:, 0:C_FOLD[1]]),
                             (cst[:, C_FOLD[1]:C_ALL], self_in_w), (w1_sb[:, :, :].rearrange("p t k -> p (t k)"), w1),
                             (b1_sb[:, :], b1), (w2_sb[:, :], w2)):
                sp.dma_start(to, what).then_inc(consts_in, 16)
            load_edges(0, 0)
            for r in (SELF_ROW, SELF_ROW + ROW):
                sp.dma_start(acc[r:r + ROW, 1, :], x_cols).then_inc(x_in, 16)
            sp.wait_ge(zeroed, 1)
            sp.dma_start(acc[:, 0, nodes_pad // 2:], acc[:, 0, 0:nodes_pad // 2]).then_inc(acc_copied, 16)

            def free_edges(n):
                at_least(sp, hid_ready, n)
                at_least(sp, msg_ready, n)

            def step(i, more):
                sp.wait_ge(gathered[0], 64 * i + 64)
                sp.wait_ge(gathered[1], 64 * i + 64)
                load_src(2 * i + 2, 0)
                free_edges(4 * i)
                load_edges(2 * i + 1, 1)
                sp.wait_ge(gathered[2], 64 * i + 64)
                sp.wait_ge(gathered[3], 64 * i + 64)
                if more:
                    load_src(2 * i + 3, 1)
                free_edges(4 * i + 2)
                load_edges(2 * i + 2, 0)

            step(0, True)
            with sp.Fori(1, n_iters - 2) as i:
                step(i, True)
            step(n_iters - 2, tail > LOAD)
            if tail > LOAD:
                free_edges(4 * n_iters - 4)
                load_edges(2 * n_iters - 1, 1)

            half = n_steps // 2
            stores = 0
            for k0, k1 in ((0, half), (half, n_steps)):
                sp.wait_ge(y_ready, k1)
                for q in range(QUARTERS):
                    row = q * quarter + k0 * NODE_STEP
                    full = min(k1 - k0, max(0, n_nodes - row) // NODE_STEP)
                    if full:
                        to = out[row:row + full * NODE_STEP, :]
                        sp.dma_start(to.rearrange("(k p j) c -> p k (j c)", k=full, p=NODE_P),
                                     y_sb[0:NODE_P, q, k0:k0 + full].rearrange("p k j c -> p k (j c)")
                                     ).then_inc(y_out, 16)
                        stores += 1
                    row += full * NODE_STEP
                    rest = min(n_nodes - row, NODE_STEP) // NODE_J if full < k1 - k0 else 0
                    if rest > 0:
                        sp.dma_start(out[row:row + rest * NODE_J, :].rearrange("(p j) c -> p (j c)", p=rest),
                                     y_sb[0:rest, q, k0 + full].rearrange("p j c -> p (j c)")).then_inc(y_out, 16)
                        stores += 1
            sp.wait_ge(y_out, 16 * stores)

        @block.gpsimd
        def _(pool):
            def step(i, first, last):
                for u in range(batches(last)):
                    at_least(pool, scaled, 4 * i + u - 3)
                    at_least(pool, prods_done, 4 * i + u - 3)
                    pool.wait_ge(src_in[u // LOAD], 16 * i + 16)
                    pool.sem_inc(turn, 1)
                    for t in range(tail_tiles if last and u == tail - 1 else TILES):
                        at = (u % LOAD) * TILES + t
                        pool.indirect_dma_start(
                            out=rows[:, u, t, :], out_offset=None, in_=x_rows,
                            in_offset=bass.IndirectOffsetOnAxis(ap=src_slot[u // LOAD][:, at:at + 1], axis=0),
                        ).then_inc(gathered[u], 16)

            iterations(pool, step)

        @block.tensor
        def _(pe):
            def hidden_layer(i, u):
                i, u = i + u // UNROLL, u % UNROLL
                slot = u // LOAD
                pe.wait_ge(feat_in[slot], 16 * i + 16)
                at_least(pe, relu_done, 4 * i + u - 1)
                at = (u % LOAD) * P
                for t in range(TILES):
                    mm = pe.matmul(hid_ps[u % 2][t % 2 * 64:t % 2 * 64 + 64, t // 2, :], w1_sb[:, t, :],
                                   feat_slot[slot][:, at:at + P], start=True, stop=True)
                mm.then_inc(hid_ready, 1)

            def edge_weights(i, u):
                i, u = i + u // UNROLL, u % UNROLL
                pe.wait_ge(relu_done, 4 * i + u + 1)
                at_least(pe, prods_done, 4 * i + u - 1)
                for t in range(TILES):
                    mm = pe.matmul(w_ps[u % 2][:, t, :], hidden[u % 2][:, t * P:(t + 1) * P],
                                   w2_sb[:, :], start=True, stop=True)
                mm.then_inc(w_ready, 1)

            def scatter(i, u, slow):
                m, hot = msg[u % 2], onehot[u % 2]
                pe.wait_ge(msg_ready, 4 * i + u + 1)
                if slow:
                    at_least(pe, acc_done, 4 * i + u)
                    for t in range(TILES):
                        to = win_ps[:, t // 2, (t % 2) * 256:(t % 2) * 256 + 256]
                        pe.matmul(to[:, 0:P], m[:, t, 0:P], eye(P), start=True, stop=True)
                        mm = pe.matmul(to[0:CHUNK_B, P:2 * P], m[:, t, P:MSG], eye(P), start=True, stop=True)
                    mm.then_inc(scattered, 1)
                    return
                pe.wait_ge(onehot_ready, 4 * i + u + 1)
                at_least(pe, acc_done, 4 * i + u - 1)
                for t in range(TILES):
                    pe.matmul(win_ps[:, u % 2, 0:WINDOW], m[:, t, 0:P], hot[:, t, :],
                              start=(t == 0), stop=(t == TILES - 1))
                for t in range(TILES):
                    mm = pe.matmul(win_ps[0:CHUNK_B, u % 2, WINDOW:2 * WINDOW], m[:, t, P:MSG], hot[:, t, :],
                                   start=(t == 0), stop=(t == TILES - 1))
                mm.then_inc(scattered, 1)

            def edges(slow):
                def step(i, first, last):
                    for u in range(batches(last)):
                        if not last or u + 1 < tail:
                            edge_weights(i, u + 1)
                        if not last or u + 2 < tail:
                            hidden_layer(i, u + 2)
                        scatter(i, u, slow)

                iterations(pe, step)

            pe.wait_ge(consts_in, 16 * 5)
            pe.wait_ge(zeroed, 6)
            hidden_layer(0, 0)
            edge_weights(0, 0)
            hidden_layer(0, 1)
            pe.wait_ge(viol_ready, 1)
            pe.matmul(win_ps[0:1, 0, 0:P], span[:, 3:4], eye(P), start=True, stop=True).then_inc(viol_row, 1)
            pe.wait_ge(flag_ready, 1)
            flag = pe.value_load(general[0:1, 0:1], min_val=0, max_val=1)
            with pe.If(flag == 0):
                edges(False)
            with pe.Else():
                edges(True)

            def fold(k):
                at_least(pe, fold_read, k - 1)
                for c in range(2):
                    for q in range(QUARTERS):
                        at = q * quarter + k * NODE_STEP
                        mm = pe.matmul(fold_ps[k % 2][q * ROW:(q + 1) * ROW, :],
                                       cst[:, C_FOLD[c]:C_FOLD[c] + ROW], acc[:, c, at:at + NODE_STEP],
                                       start=(c == 0), stop=(c == 1))
                mm.then_inc(folded, 1)

            def turn(k):
                pe.wait_ge(fold_read, k + 1)
                at_least(pe, centres, k - 1)
                for j in range(NODE_J):
                    mm = pe.transpose(node_ps[k % 2][0:NODE_P, j * P:(j + 1) * P],
                                      by_column[k % 2][:, j:NODE_STEP:NODE_J], eye(P))
                mm.then_inc(turned, 1)

            pe.wait_ge(checked, 6)
            pe.wait_ge(acc_done, n_batches)
            fold(0)
            for k in range(n_steps):
                if k + 1 < n_steps:
                    fold(k + 1)
                turn(k)

        @block.scalar
        def _(act):
            act.wait_ge(zeroed, 2)
            act.activation(acc[0:SELF_ROW, 1, :], zero_row[0:SELF_ROW, 0:1].broadcast_to([SELF_ROW, nodes_pad]),
                           ACT.Copy).then_inc(acc_zeroed, 1)

            def relu(i, u):
                i, u = i + u // UNROLL, u % UNROLL
                act.wait_ge(hid_ready, 4 * i + u + 1)
                at_least(act, w_ready, 4 * i + u - 1)
                for h in range(2):
                    op = act.activation(hidden[u % 2][0:64, :].rearrange("k (t h e) -> k t h e", t=2, h=2)[:, :, h, :],
                                        hid_ps[u % 2][64 * h:64 * h + 64, :, :], ACT.Relu,
                                        bias=b1_sb[64 * h:64 * h + 64, 0:1])
                op.then_inc(relu_done, 1)

            def scale_rows(i, u, last=False):
                i, u = i + u // UNROLL, u % UNROLL
                act.wait_ge(gathered[u], rows_there(i, u, last))
                if u % LOAD == 0:
                    act.wait_ge(sh_in[u // LOAD], 16 * i + 16)
                at_least(act, prods_done, 4 * i + u - 1)
                for t in range(TILES):
                    op = act.activation(inputs[u % 2][:, t, 0:ROW], rows[:, u, t, :], ACT.Copy,
                                        scale=sh_slot[u // LOAD][:, u % LOAD, t, 0:1])
                op.then_inc(scaled, 1)

            def distances(i, u):
                at_least(act, onehot_ready, 4 * i + u)
                for t in range(TILES):
                    op = act.activation(dist[:, t, :], iota, ACT.Abs,
                                        bias=neg_local[:, bass.ds((4 * i + u) * TILES + t, 1)])
                op.then_inc(dist_done, 1)

            def one_hot(i, u):
                act.wait_ge(dist_done, 4 * i + u + 1)
                at_least(act, scattered, 4 * i + u - 1)
                act.activation(onehot[u % 2][:, :, :], dist[:, :, :], ACT.Relu,
                               bias=one_col[:, 0:1], scale=-1.0).then_inc(onehot_ready, 1)

            def edges(slow):
                def step(i, first, last):
                    for u in range(batches(last)):
                        more = not last or u + 1 < tail
                        if more:
                            relu(i, u + 1)
                        if not slow:
                            distances(i, u)
                        if more:
                            scale_rows(i, u + 1, last)
                        if not slow:
                            one_hot(i, u)

                iterations(act, step)

            act.wait_ge(consts_in, 16 * 5)
            relu(0, 0)
            scale_rows(0, 0)
            act.wait_ge(flag_ready, 1)
            flag = act.value_load(general[0:1, 0:1], min_val=0, max_val=1)
            with act.If(flag == 0):
                edges(False)
            with act.Else():
                edges(True)

            def read_fold(k):
                act.wait_ge(folded, k + 1)
                at_least(act, turned, k - 1)
                act.activation(by_column[k % 2][:, :], fold_ps[k % 2], ACT.Copy).then_inc(fold_read, 1)

            def square(k):
                act.wait_ge(centres, k + 1)
                at_least(act, squares_summed, k - 1)
                act.activation(squares[k % 2][0:NODE_P, :, :], centred[0:NODE_P, k, :, :],
                               ACT.Square).then_inc(squared, 1)

            read_fold(0)
            for k in range(n_steps):
                if k + 1 < n_steps:
                    read_fold(k + 1)
                square(k)
            act.wait_ge(squares_summed, n_steps)
            act.activation(spread[0:NODE_P, 1], spread[0:NODE_P, 0], ACT.Sqrt, bias=eps_col[0:NODE_P, 0:1],
                           scale=1.0 / ROW).then_inc(rooted, 1)

        @block.vector
        def _(dve):
            dve.memset(acc[:, 0, 0:nodes_pad // 2], 0.0).then_inc(zeroed, 1)
            dve.memset(zero_row[:, :], 0.0).then_inc(zeroed, 1)
            for s in range(2):
                dve.memset(hidden[s][64:P, :], 0.0).then_inc(zeroed, 1)
            dve.wait_ge(zeroed, 4)
            for s in range(2):
                dve.memset(hidden[s][64:65, :], 1.0).then_inc(zeroed, 1)
            dve.memset(one_col[:, :], 1.0).then_inc(zeroed, 1)
            dve.memset(eps_col[:, :], EPS).then_inc(zeroed, 1)
            dve.memset(win_ps[:, :, :], 0.0).then_inc(zeroed, 1)

            dve.wait_ge(dst_in, 32)
            dve.tensor_tensor(neg_local[:, :].rearrange("p (b t) -> p b t", t=TILES),
                              first_sb[:, :].unsqueeze(2).broadcast_to([P, padded, TILES]),
                              dst_sb[:, :].rearrange("p (b t) -> p b t", t=TILES),
                              ALU.subtract).then_inc(checked, 1)
            dve.wait_ge(checked, 1)
            dve.tensor_reduce(span[:, 0:1], neg_local[:, :], AX_X, ALU.max).then_inc(checked, 1)
            dve.tensor_reduce(span[:, 1:2], neg_local[:, :], AX_X, ALU.min).then_inc(checked, 1)
            dve.wait_ge(checked, 3)
            dve.tensor_scalar(span[:, 2:3], span[:, 1:2], -1.0, float(1 - WINDOW), ALU.mult, ALU.add).then_inc(checked, 1)
            dve.wait_ge(checked, 4)
            dve.wait_ge(zeroed, 9)
            dve.tensor_tensor(span[:, 3:4], span[:, 0:1], span[:, 2:3], ALU.max).then_inc(viol_ready, 1)
            dve.wait_ge(viol_row, 1)
            dve.tensor_reduce(worst[:, 0:1], win_ps[0:1, 0, 0:P], AX_X, ALU.max).then_inc(checked, 1)
            dve.wait_ge(checked, 5)
            dve.tensor_scalar(general[:, :], worst[:, 0:1], 0.0, None, ALU.is_gt).then_inc(flag_ready, 1)
            dve.wait_ge(consts_in, 16 * 5)
            self_w = cst[SELF_ROW:SELF_ROW + ROW, C_FOLD[1]:C_FOLD[1] + ROW]
            dve.tensor_scalar(self_w, self_w, float(MUL) ** -0.5, None, ALU.mult).then_inc(checked, 1)

            def messages(i, u, last):
                g = 4 * i + u
                shv = sh_slot[u // LOAD][:, u % LOAD, :, :]
                r, y, w, m = rows[:, u, :, :], inputs[u % 2], w_ps[u % 2], msg[u % 2]
                at_least(dve, msg_ready, g)
                dve.wait_ge(gathered[u], rows_there(i, u, last))
                if u % LOAD == 0:
                    dve.wait_ge(sh_in[u // LOAD], 16 * i + 16)
                dve.tensor_tensor(v_sh1[:, :, :, :], r[:, :, 0:S_COL].rearrange("p t (m i) -> p t m i", m=3),
                                  shv[:, :, 1:4].unsqueeze(3).broadcast_to([P, TILES, 3, MUL]),
                                  ALU.mult).then_inc(v_sh1_done, 1)
                dve.wait_ge(w_ready, g + 1)
                dve.tensor_tensor(prod_s[:, :, :, :],
                                  w[:, :, W011:W_ALL].rearrange("p t (i o) -> p t i o", o=MUL),
                                  r[:, :, S_COL:ROW].unsqueeze(3).broadcast_to([P, TILES, MUL, MUL]),
                                  ALU.mult).then_inc(prod_s_done, 1)
                dve.wait_ge(v_sh1_done, g + 1)
                dve.tensor_reduce(y[:, :, B_COL:B_COL + MUL], v_sh1[:, :, :, :].rearrange("p t m i -> p t i m"),
                                  AX_X, ALU.add).then_inc(b_done, 1)
                dve.wait_ge(scaled, g + 1)
                dve.tensor_tensor(
                    prod[:, :, 0:3, :].rearrange("p t m (i o) -> p t m i o", o=MUL),
                    w[:, :, W101:W000].rearrange("p t (i o) -> p t i o", o=MUL).unsqueeze(2)
                    .broadcast_to([P, TILES, 3, MUL, MUL]),
                    y[:, :, 0:S_COL].rearrange("p t (m i) -> p t m i", m=3).unsqueeze(4)
                    .broadcast_to([P, TILES, 3, MUL, MUL]), ALU.mult).then_inc(prod_v_done, 1)
                dve.wait_ge(b_done, g + 1)
                dve.tensor_tensor(
                    prod[:, :, 3:5, :].rearrange("p t b (i o) -> p t (b i) o", o=MUL),
                    w[:, :, W000:W011].rearrange("p t (i o) -> p t i o", o=MUL),
                    y[:, :, S_COL:ROW + MUL].unsqueeze(3).broadcast_to([P, TILES, 2 * MUL, MUL]),
                    ALU.mult).then_inc(prods_done, 1)
                dve.wait_ge(prod_s_done, g + 1)
                dve.tensor_reduce(sum_s[:, :, :], prod_s[:, :, :, :].rearrange("p t i o -> p t o i"),
                                  AX_X, ALU.add).then_inc(sum_s_done, 1)
                dve.wait_ge(prod_v_done, g + 1)
                dve.wait_ge(prods_done, g + 1)
                at_least(dve, scattered, g - 1)
                dve.tensor_tensor(m[:, :, 0:T_COL].rearrange("p t (b c) -> p t b c", c=HALF),
                                  prod[:, :, :, 0:HALF], prod[:, :, :, HALF:2 * HALF],
                                  ALU.add).then_inc(halves_done, 1)
                dve.wait_ge(sum_s_done, g + 1)
                dve.tensor_tensor(m[:, :, T_COL:MSG].rearrange("p t (m o) -> p t m o", m=3),
                                  sum_s[:, :, :].unsqueeze(2).broadcast_to([P, TILES, 3, MUL]),
                                  shv[:, :, 1:4].unsqueeze(3).broadcast_to([P, TILES, 3, MUL]),
                                  ALU.mult).then_inc(msg_ready, 1)

            def accumulate(i, u, slow):
                g = 4 * i + u
                if slow:
                    n = g + 1 if isinstance(g, int) else dve.snap(g + 1)
                    dve.wait_ge(flag_ready, 1)
                    dve.wait_ge(scattered, n)
                    for t in range(TILES):
                        col = (t % 2) * 256
                        with dve.Fori(0, P) as e:
                            node = dve.value_load(dst_rows[:, bass.ds(g * BATCH + t * P + e, 1)],
                                                  min_val=0, max_val=n_nodes - 1)
                            to = acc[:, :, bass.ds(node, 1)]
                            column = win_ps[:, t // 2, bass.ds(e + col, P + 1)][:, 0:P + 1:P].unsqueeze(2)
                            dve.tensor_tensor(to, to, column, ALU.add)
                            dve.drain()
                    dve.sem_inc(acc_done, 1)
                    return
                node = dve.value_load(first_sb[0:1, bass.ds(g, 1)], min_val=0, max_val=n_nodes - 1)
                at_least(dve, acc_done, g)
                dve.wait_ge(scattered, g + 1)
                to = acc[:, :, bass.ds(node, WINDOW)]
                dve.tensor_tensor(to, to, win_ps[:, u % 2, 0:2 * WINDOW].rearrange("p (c n) -> p c n", c=2),
                                  ALU.add).then_inc(acc_done, 1)

            def edges(slow):
                dve.wait_ge(acc_zeroed, 1)
                dve.wait_ge(acc_copied, 16)
                dve.wait_ge(x_in, 32)

                def step(i, first, last):
                    for u in range(batches(last)):
                        messages(i, u, last)
                        if not first or u > 0:
                            accumulate(i, u - 1, slow)

                iterations(dve, step)
                accumulate(n_iters - 1, tail - 1, slow)

            dve.wait_ge(flag_ready, 1)
            flag = dve.value_load(general[0:1, 0:1], min_val=0, max_val=1)
            with dve.If(flag == 0):
                edges(False)
            with dve.Else():
                edges(True)

            def centre(k):
                ps = node_ps[k % 2][0:NODE_P, :].rearrange("p (g c) -> p g c", c=ROW)
                dve.wait_ge(turned, k + 1)
                dve.tensor_reduce(total[0:NODE_P, k, :], ps, AX_X, ALU.add).then_inc(totals, 1)
                dve.wait_ge(totals, k + 1)
                dve.scalar_tensor_tensor(
                    out=centred[0:NODE_P, k, :, :],
                    in0=total[0:NODE_P, k, :].unsqueeze(2).broadcast_to([NODE_P, GROUPS, ROW]),
                    scalar=-1.0 / ROW, in1=ps, op0=ALU.mult, op1=ALU.add).then_inc(centres, 1)

            def sum_squares(k):
                dve.wait_ge(squared, k + 1)
                dve.tensor_reduce(spread[0:NODE_P, 0, k, :], squares[k % 2][0:NODE_P, :, :], AX_X,
                                  ALU.add).then_inc(squares_summed, 1)

            centre(0)
            for k in range(n_steps):
                if k + 1 < n_steps:
                    centre(k + 1)
                sum_squares(k)
            dve.wait_ge(rooted, 1)
            dve.reciprocal(spread[0:NODE_P, 2], spread[0:NODE_P, 1]).then_inc(inverted, 1)
            dve.wait_ge(inverted, 1)
            for k in range(n_steps):
                dve.tensor_tensor(
                    y_sb[0:NODE_P, :, k, :, :].rearrange("p q j c -> p j q c"),
                    centred[0:NODE_P, k, :, :].rearrange("p (j q) c -> p j q c", j=NODE_J),
                    spread[0:NODE_P, 2, k, :].rearrange("p (j q) -> p j q", j=NODE_J).unsqueeze(3)
                    .broadcast_to([NODE_P, NODE_J, QUARTERS, ROW]), ALU.mult).then_inc(y_ready, 1)


def constants():
    import numpy as np

    c = np.zeros((P, C_ALL), np.float32)
    c[:, C_EYE:C_EYE + P] = np.eye(P, dtype=np.float32)
    c[:, C_IOTA:C_IOTA + WINDOW] = np.arange(WINDOW, dtype=np.float32)
    c110 = 1.0 / np.sqrt(3.0)
    for o in range(MUL):
        for part in range(MUL // 2):
            for m in range(3):
                c[m * HALF + part * MUL + o, C_FOLD[0] + MUL + 3 * o + m] = ALPHA
            c[3 * HALF + part * MUL + o, C_FOLD[0] + o] = ALPHA
            c[part * MUL + o, C_FOLD[1] + o] = ALPHA * c110
        for m in range(3):
            c[HALF + m * MUL + o, C_FOLD[1] + MUL + 3 * o + m] = ALPHA
            c[SELF_ROW + ROW + m * MUL + o, C_FOLD[1] + MUL + 3 * o + m] = 1.0
        c[SELF_ROW + ROW + S_COL + o, C_FOLD[1] + o] = 1.0
    return c


def layouts(x, src, dst, edge_attr_32, edge_attr_4, L0_gnn_W1, L0_gnn_b1, L0_gnn_W2, L0_gnn_b2,
            L0_gnn_si_w0, L0_gnn_si_w1):
    import numpy as np

    x, src, dst, feat, sh = (np.asarray(a) for a in (x, src, dst, edge_attr_32, edge_attr_4))
    n, e = x.shape[0], src.shape[0]
    batches = -(-e // (LOAD * BATCH)) * LOAD
    pad = batches * BATCH - e
    steps = -(-(n + WINDOW) // (QUARTERS * NODE_STEP))
    src = np.pad(src, (0, pad), mode="edge")
    dst = np.pad(dst, (0, pad), mode="edge")
    feat = np.pad(feat, ((0, pad), (0, 0)))
    sh = np.pad(sh, ((0, pad), (0, 0)))
    x_rows = np.concatenate([x[:, 8:].reshape(n, 8, 3).transpose(0, 2, 1).reshape(n, 24), x[:, :8]], axis=1)
    more = steps * QUARTERS * NODE_STEP - n
    w2 = np.asarray(L0_gnn_W2).reshape(64, 4, 64)[:, [2, 0, 3, 1]].reshape(64, 256)
    b2 = np.asarray(L0_gnn_b2).reshape(1, 4, 64)[:, [2, 0, 3, 1]].reshape(1, 256)
    w1 = np.zeros((TILES, 32, TILES, 64), x.dtype)
    for t in range(TILES):
        w1[t, :, t] = np.asarray(L0_gnn_W1)
    w2 = np.pad(np.concatenate([w2, b2]), ((0, P - 65), (0, 0)))
    consts = constants()
    fold_b = consts[:, C_FOLD[1]:].copy()
    self_w = fold_b[SELF_ROW:SELF_ROW + ROW]
    self_w[24:, :8] = np.asarray(L0_gnn_si_w0)
    for m in range(3):
        self_w[8 * m:8 * m + 8, 8 + m::3] = np.asarray(L0_gnn_si_w1)
    return {
        "x_rows": x_rows,
        "x_cols": np.pad(x_rows, ((0, more), (0, 0))).T,
        "src": src.reshape(batches * TILES, P).T,
        "dst": dst.reshape(batches * TILES, P).T,
        "dst_first": dst[::BATCH].reshape(1, batches),
        "dst_rows": dst.reshape(1, -1),
        "feat": feat.reshape(batches, TILES, P, 32).transpose(1, 3, 0, 2).reshape(P, -1),
        "sh": sh.reshape(batches * TILES, P, 4).transpose(1, 0, 2).reshape(P, -1),
        "w1": w1.reshape(P, -1),
        "b1": np.tile(np.asarray(L0_gnn_b1), 2).reshape(P, 1),
        "w2": w2,
        "self_in_w": fold_b,
        "consts": consts,
    }


def kernel(**inputs):
    import numpy as np
    import concourse.bacc as bacc
    from concourse.bass_utils import run_bass_kernel_spmd

    nc = bacc.Bacc("TRN2", target_bir_lowering=False, num_devices=1)
    arrays = {k: np.ascontiguousarray(a) for k, a in layouts(**inputs).items()}
    args = {k: nc.dram_tensor(f"{k}_dram", a.shape, mybir.dt.from_np(a.dtype), kind="ExternalInput").ap()
            for k, a in arrays.items()}
    out = nc.dram_tensor("out_dram", inputs["x"].shape, F32, kind="ExternalOutput").ap()
    build(nc, out=out, n_tiles=-(-inputs["src"].shape[0] // P), **args)
    r = run_bass_kernel_spmd(nc, [{f"{k}_dram": a for k, a in arrays.items()}], core_ids=[0])
    return r.results[0]["out_dram"]
```

```python
from contextlib import ExitStack

import concourse.bass as bass
from concourse import mybir

P = 128
F32 = mybir.dt.float32
I32 = mybir.dt.int32
ALU = mybir.AluOpType
ACT = mybir.ActivationFunctionType
AX_X = mybir.AxisListType.X

MUL = 8
TILES = 4
BATCH = TILES * P
UNROLL = 8
LOAD = UNROLL // 2
WINDOW = 64
HALF = MUL // 2 * MUL
QUARTERS = 4
NODE_P, NODE_J = 100, 4
NODE_STEP = NODE_P * NODE_J
GROUPS = QUARTERS * NODE_J
SELF_ROW = 64
ALPHA = 0.25
EPS = 1e-5

W101, W000, W110, W011, W_ALL = 0, 64, 128, 192, 256
S_COL, ROW = 3 * MUL, 4 * MUL
B_COL = ROW
T_COL = 5 * HALF
MSG = T_COL + 3 * MUL
CHUNK_B = MSG - P
C_EYE, C_IOTA, C_FOLD, C_ALL = 0, 128, (192, 224), 256


def at_least(eng, sem, value):
    if not isinstance(value, int) or value > 0:
        eng.wait_ge(sem, value)


def build(nc, x_rows, x_cols, src, dst, dst_first, dst_rows, feat, sh, w1, b1, w2,
          self_in_w, consts, out, n_tiles):
    n_nodes = out.shape[0]
    n_batches = -(-n_tiles // TILES)
    padded = dst_first.shape[1]
    n_iters = -(-n_batches // UNROLL)
    tail = n_batches - UNROLL * (n_iters - 1)
    tail_tiles = n_tiles - TILES * (n_batches - 1)
    nodes_pad = x_cols.shape[1]
    quarter = nodes_pad // QUARTERS
    n_steps = quarter // NODE_STEP
    assert n_iters >= 4 and n_steps >= 4 and tail >= 2 and 1 <= tail_tiles <= TILES
    assert nodes_pad == QUARTERS * n_steps * NODE_STEP >= n_nodes + WINDOW

    with ExitStack() as ctx:
        def sb(name, shape, dt=F32):
            return ctx.enter_context(nc.sbuf_tensor(name, shape, dt))

        def psum(name, shape):
            return ctx.enter_context(nc.psum_tensor(name, shape, F32))

        def sem(name):
            return ctx.enter_context(nc.semaphore(name))

        cst = sb("cst", [P, C_ALL])
        w1_sb = sb("w1_sb", [P, TILES, 64])
        b1_sb = sb("b1_sb", [P, 1])
        w2_sb = sb("w2_sb", [P, W_ALL])
        zero_row = sb("zero_row", [P, 1])
        one_col = sb("one_col", [P, 1])
        eps_col = sb("eps_col", [P, 1])
        dst_sb = sb("dst_sb", [P, padded * TILES], I32)
        first_sb = sb("first_sb", [P, padded], I32)
        neg_local = sb("neg_local", [P, padded * TILES])
        span = sb("span", [P, 4])
        worst = sb("worst", [1, 2])
        general = sb("general", [1, 1], I32)
        src_slot = [sb(f"src_slot{s}", [P, LOAD * TILES], I32) for s in range(2)]
        feat_slot = [sb(f"feat_slot{s}", [P, LOAD * P]) for s in range(2)]
        sh_slot = [sb(f"sh_slot{s}", [P, LOAD, TILES, 4]) for s in range(2)]
        rows = sb("rows", [P, UNROLL, TILES, ROW])
        hidden = [sb(f"hidden{s}", [P, BATCH]) for s in range(2)]
        inputs = [sb(f"inputs{s}", [P, TILES, ROW + MUL]) for s in range(2)]
        v_sh1 = sb("v_sh1", [P, TILES, 3, MUL])
        prod = sb("prod", [P, TILES, 5, MUL * MUL])
        prod_s = sb("prod_s", [P, TILES, MUL, MUL])
        sum_s = sb("sum_s", [P, TILES, MUL])
        msg = [sb(f"msg{s}", [P, TILES, MSG]) for s in range(2)]
        dist = sb("dist", [P, TILES, WINDOW])
        onehot = [sb(f"onehot{s}", [P, TILES, WINDOW]) for s in range(2)]
        acc = sb("acc", [P, 2, nodes_pad])
        fold_sum = sb("fold_sum", [P, 2])
        by_column = [sb(f"by_column{s}", [P, NODE_STEP]) for s in range(2)]
        squares = [sb(f"squares{s}", [P, GROUPS, ROW]) for s in range(2)]
        sum_sq = sb("sum_sq", [P, n_steps, GROUPS])
        deviation = sb("deviation", [P, n_steps, GROUPS])
        inverse = sb("inverse", [P, n_steps, GROUPS])
        first_root = sb("first_root", [P, 1])
        y_sb = sb("y_sb", [P, n_steps, QUARTERS, NODE_J * ROW])

        hid_ps = [psum(f"hid_ps{s}", [P, 2, P]) for s in range(2)]
        w_ps = [psum(f"w_ps{s}", [P, TILES, W_ALL]) for s in range(2)]
        win_ps = psum("win_ps", [P, 2, 512])

        consts_in = sem("consts_in")
        dst_in = sem("dst_in")
        src_in = [sem(f"src_in{s}") for s in range(2)]
        feat_in = [sem(f"feat_in{s}") for s in range(2)]
        sh_in = [sem(f"sh_in{s}") for s in range(2)]
        gathered = [sem(f"gathered{u}") for u in range(UNROLL)]
        turn = sem("turn")
        zeroed = sem("zeroed")
        acc_zeroed = sem("acc_zeroed")
        checked = sem("checked")
        flag_ready = sem("flag_ready")
        viol_ready = sem("viol_ready")
        viol_row = sem("viol_row")
        hid_ready = sem("hid_ready")
        relu_done = sem("relu_done")
        w_ready = sem("w_ready")
        scaled = sem("scaled")
        dist_done = sem("dist_done")
        onehot_ready = sem("onehot_ready")
        v_sh1_done = sem("v_sh1_done")
        prod_v_done = sem("prod_v_done")
        b_done = sem("b_done")
        prod_s_done = sem("prod_s_done")
        prods_done = sem("prods_done")
        sum_s_done = sem("sum_s_done")
        msg_ready = sem("msg_ready")
        scattered = sem("scattered")
        acc_done = sem("acc_done")
        acc_copied = sem("acc_copied")
        fold_centred = sem("fold_centred")
        x_in = sem("x_in")
        folded = sem("folded")
        fold_read = sem("fold_read")
        turned = sem("turned")
        squared = sem("squared")
        squares_summed = sem("squares_summed")
        rooted = sem("rooted")
        inverted = sem("inverted")
        y_ready = sem("y_ready")
        y_out = sem("y_out")

        block = ctx.enter_context(nc.Block())

        def eye(n):
            return cst[:, C_EYE:C_EYE + n]

        iota = cst[:, C_IOTA:C_IOTA + WINDOW]

        def iterations(eng, step):
            step(0, True, False)
            with eng.Fori(1, n_iters - 1) as i:
                step(i, False, False)
            step(n_iters - 1, False, True)

        def batches(last):
            return tail if last else UNROLL

        def tiles(u, last):
            return tail_tiles if last and u == tail - 1 else TILES

        banks = [w_ps[s][:, 2 * h:2 * h + 2, :].rearrange("p t c -> p (t c)") for s in range(2) for h in range(2)]
        fold_ps = [bank[:, 0:NODE_STEP] for bank in banks[0:2]]
        node_ps = [bank[0:NODE_P, :] for bank in (*banks[2:4], win_ps[:, 0, :], win_ps[:, 1, :])]

        @block.sync
        def _(sp):
            def load_src(k, s):
                w = LOAD * TILES
                sp.dma_start(src_slot[s][:, :], src[:, bass.ds(k * w, w)]).then_inc(src_in[s], 16)

            def load_edges(k, s):
                w = LOAD * P
                sp.dma_start(feat_slot[s][:, :], feat[:, bass.ds(k * w, w)]).then_inc(feat_in[s], 16)
                w = LOAD * TILES * 4
                sp.dma_start(sh_slot[s][:, :, :, :].rearrange("p b t c -> p (b t c)"),
                             sh[:, bass.ds(k * w, w)]).then_inc(sh_in[s], 16)

            load_src(0, 0)
            load_src(1, 1)
            sp.dma_start(dst_sb[:, :], dst).then_inc(dst_in, 16)
            sp.dma_start(first_sb[:, :], dst_first.broadcast_to([P, padded])).then_inc(dst_in, 16)
            for to, what in ((cst[:, 0:C_FOLD[1]], consts[:, 0:C_FOLD[1]]),
                             (cst[:, C_FOLD[1]:C_ALL], self_in_w), (w1_sb[:, :, :].rearrange("p t k -> p (t k)"), w1),
                             (b1_sb[:, :], b1), (w2_sb[:, :], w2)):
                sp.dma_start(to, what).then_inc(consts_in, 16)
            load_edges(0, 0)
            for r in (SELF_ROW, SELF_ROW + ROW):
                sp.dma_start(acc[r:r + ROW, 1, :], x_cols).then_inc(x_in, 16)
            sp.wait_ge(zeroed, 1)
            sp.dma_start(acc[:, 0, nodes_pad // 2:], acc[:, 0, 0:nodes_pad // 2]).then_inc(acc_copied, 16)

            def free_edges(n):
                at_least(sp, hid_ready, n)
                at_least(sp, msg_ready, n)

            def step(i, more):
                free_edges(UNROLL * i)
                load_edges(2 * i + 1, 1)
                for u in range(LOAD):
                    sp.wait_ge(gathered[u], 64 * i + 64)
                load_src(2 * i + 2, 0)
                free_edges(UNROLL * i + LOAD)
                load_edges(2 * i + 2, 0)
                if more:
                    for u in range(LOAD, UNROLL):
                        sp.wait_ge(gathered[u], 64 * i + 64)
                    load_src(2 * i + 3, 1)

            step(0, True)
            with sp.Fori(1, n_iters - 2) as i:
                step(i, True)
            step(n_iters - 2, tail > LOAD)
            if tail > LOAD:
                free_edges(UNROLL * (n_iters - 1))
                load_edges(2 * n_iters - 1, 1)

            whole = n_nodes // quarter
            stores = 0
            for k in range(n_steps):
                sp.wait_ge(y_ready, k + 1)
                to = out[0:whole * quarter, :].rearrange("(q k p j) c -> k p q (j c)", q=whole, k=n_steps, p=NODE_P)
                sp.dma_start(to[k], y_sb[0:NODE_P, k, 0:whole, :]).then_inc(y_out, 16)
                stores += 1
                for q in range(whole, QUARTERS):
                    row = q * quarter + k * NODE_STEP
                    rest = min(n_nodes - row, NODE_STEP)
                    if rest > 0:
                        sp.dma_start(out[row:row + rest, :].rearrange("(p j) c -> p (j c)", j=NODE_J),
                                     y_sb[0:rest // NODE_J, k, q, :]).then_inc(y_out, 16)
                        stores += 1
            sp.wait_ge(y_out, 16 * stores)

        @block.gpsimd
        def _(pool):
            def step(i, first, last):
                for u in range(batches(last)):
                    at_least(pool, scaled, UNROLL * (i - 1) + u + 1)
                    at_least(pool, prods_done, UNROLL * (i - 1) + u + 1)
                    pool.wait_ge(src_in[u // LOAD], 16 * i + 16)
                    pool.sem_inc(turn, 1)
                    for t in range(tiles(u, last)):
                        at = (u % LOAD) * TILES + t
                        pool.indirect_dma_start(
                            out=rows[:, u, t, :], out_offset=None, in_=x_rows,
                            in_offset=bass.IndirectOffsetOnAxis(ap=src_slot[u // LOAD][:, at:at + 1], axis=0),
                        ).then_inc(gathered[u], 16)

            iterations(pool, step)

        @block.tensor
        def _(pe):
            def hidden_layer(i, u):
                i, u = i + u // UNROLL, u % UNROLL
                slot = u // LOAD
                pe.wait_ge(feat_in[slot], 16 * i + 16)
                at_least(pe, relu_done, UNROLL * i + u - 1)
                at = (u % LOAD) * P
                for t in range(TILES):
                    mm = pe.matmul(hid_ps[u % 2][t % 2 * 64:t % 2 * 64 + 64, t // 2, :], w1_sb[:, t, :],
                                   feat_slot[slot][:, at:at + P], start=True, stop=True)
                mm.then_inc(hid_ready, 1)

            def edge_weights(i, u, n=TILES):
                i, u = i + u // UNROLL, u % UNROLL
                pe.wait_ge(relu_done, UNROLL * i + u + 1)
                at_least(pe, prods_done, UNROLL * i + u - 1)
                for t in range(n):
                    mm = pe.matmul(w_ps[u % 2][:, t, :], hidden[u % 2][:, t * P:(t + 1) * P],
                                   w2_sb[:, :], start=True, stop=True)
                mm.then_inc(w_ready, 1)

            def scatter(i, u, n, slow):
                m, hot = msg[u % 2], onehot[u % 2]
                pe.wait_ge(msg_ready, UNROLL * i + u + 1)
                if slow:
                    at_least(pe, acc_done, UNROLL * i + u)
                    for t in range(n):
                        to = win_ps[:, t // 2, (t % 2) * 256:(t % 2) * 256 + 256]
                        pe.matmul(to[:, 0:P], m[:, t, 0:P], eye(P), start=True, stop=True)
                        mm = pe.matmul(to[0:CHUNK_B, P:2 * P], m[:, t, P:MSG], eye(P), start=True, stop=True)
                    mm.then_inc(scattered, 1)
                    return
                pe.wait_ge(onehot_ready, UNROLL * i + u + 1)
                at_least(pe, acc_done, UNROLL * i + u - 1)
                for t in range(n):
                    pe.matmul(win_ps[:, u % 2, 0:WINDOW], m[:, t, 0:P], hot[:, t, :],
                              start=(t == 0), stop=(t == n - 1))
                for t in range(n):
                    mm = pe.matmul(win_ps[0:CHUNK_B, u % 2, WINDOW:2 * WINDOW], m[:, t, P:MSG], hot[:, t, :],
                                   start=(t == 0), stop=(t == n - 1))
                mm.then_inc(scattered, 1)

            def edges(slow):
                def step(i, first, last):
                    for u in range(batches(last)):
                        if not last or u + 1 < tail:
                            edge_weights(i, u + 1, tiles(u + 1, last))
                        if not last or u + 2 < tail:
                            hidden_layer(i, u + 2)
                        scatter(i, u, tiles(u, last), slow)

                iterations(pe, step)

            pe.wait_ge(consts_in, 16 * 5)
            pe.wait_ge(zeroed, 6)
            hidden_layer(0, 0)
            edge_weights(0, 0)
            hidden_layer(0, 1)
            pe.wait_ge(viol_ready, 1)
            pe.matmul(win_ps[0:1, 0, 0:P], span[:, 3:4], eye(P), start=True, stop=True).then_inc(viol_row, 1)
            pe.wait_ge(flag_ready, 1)
            flag = pe.value_load(general[0:1, 0:1], min_val=0, max_val=1)
            with pe.If(flag == 0):
                edges(False)
            with pe.Else():
                edges(True)

            def fold(k):
                at_least(pe, fold_read, k - 1)
                for c in range(2):
                    for q in range(QUARTERS):
                        at = q * quarter + k * NODE_STEP
                        mm = pe.matmul(fold_ps[k % 2][q * ROW:(q + 1) * ROW, :],
                                       cst[:, C_FOLD[c]:C_FOLD[c] + ROW], acc[:, c, at:at + NODE_STEP],
                                       start=(c == 0), stop=(c == 1))
                mm.then_inc(folded, 1)

            def turn_step(k):
                pe.wait_ge(fold_read, k + 1)
                at_least(pe, y_ready, k - 3)
                for j in range(NODE_J):
                    mm = pe.transpose(node_ps[k % 4][:, j * P:(j + 1) * P],
                                      by_column[k % 2][:, j:NODE_STEP:NODE_J], eye(P))
                mm.then_inc(turned, 1)

            pe.wait_ge(fold_centred, 1)
            pe.wait_ge(acc_done, n_batches)
            fold(0)
            for k in range(n_steps):
                if k + 1 < n_steps:
                    fold(k + 1)
                turn_step(k)

        @block.scalar
        def _(act):
            act.wait_ge(zeroed, 2)
            act.activation(acc[0:SELF_ROW, 1, :], zero_row[0:SELF_ROW, 0:1].broadcast_to([SELF_ROW, nodes_pad]),
                           ACT.Copy).then_inc(acc_zeroed, 1)

            def relu(i, u):
                i, u = i + u // UNROLL, u % UNROLL
                act.wait_ge(hid_ready, UNROLL * i + u + 1)
                at_least(act, w_ready, UNROLL * i + u - 1)
                for h in range(2):
                    op = act.activation(hidden[u % 2][0:64, :].rearrange("k (t h e) -> k t h e", t=2, h=2)[:, :, h, :],
                                        hid_ps[u % 2][64 * h:64 * h + 64, :, :], ACT.Relu,
                                        bias=b1_sb[64 * h:64 * h + 64, 0:1])
                op.then_inc(relu_done, 1)

            def scale_rows(i, u, n=TILES):
                i, u = i + u // UNROLL, u % UNROLL
                act.wait_ge(gathered[u], 64 * i + 16 * n)
                if u % LOAD == 0:
                    act.wait_ge(sh_in[u // LOAD], 16 * i + 16)
                at_least(act, prods_done, UNROLL * i + u - 1)
                for t in range(n):
                    op = act.activation(inputs[u % 2][:, t, 0:ROW], rows[:, u, t, :], ACT.Copy,
                                        scale=sh_slot[u // LOAD][:, u % LOAD, t, 0:1])
                op.then_inc(scaled, 1)

            def distances(i, u, n):
                at_least(act, onehot_ready, UNROLL * i + u)
                for t in range(n):
                    op = act.activation(dist[:, t, :], iota, ACT.Abs,
                                        bias=neg_local[:, bass.ds((UNROLL * i + u) * TILES + t, 1)])
                op.then_inc(dist_done, 1)

            def one_hot(i, u, n):
                act.wait_ge(dist_done, UNROLL * i + u + 1)
                at_least(act, scattered, UNROLL * i + u - 1)
                act.activation(onehot[u % 2][:, 0:n, :], dist[:, 0:n, :], ACT.Relu,
                               bias=one_col[:, 0:1], scale=-1.0).then_inc(onehot_ready, 1)

            def edges(slow):
                def step(i, first, last):
                    for u in range(batches(last)):
                        more = not last or u + 1 < tail
                        if more:
                            relu(i, u + 1)
                        if not slow:
                            distances(i, u, tiles(u, last))
                        if more:
                            scale_rows(i, u + 1, tiles(u + 1, last))
                        if not slow:
                            one_hot(i, u, tiles(u, last))

                iterations(act, step)

            act.wait_ge(consts_in, 16 * 5)
            relu(0, 0)
            scale_rows(0, 0)
            act.wait_ge(flag_ready, 1)
            flag = act.value_load(general[0:1, 0:1], min_val=0, max_val=1)
            with act.If(flag == 0):
                edges(False)
            with act.Else():
                edges(True)

            act.wait_ge(zeroed, 9)
            act.activation(first_root[:, :], eps_col[:, :], ACT.Sqrt)

            def read_fold(k):
                act.wait_ge(folded, k + 1)
                at_least(act, turned, k - 1)
                act.activation(by_column[k % 2][:, :], fold_ps[k % 2], ACT.Copy).then_inc(fold_read, 1)

            def square(k):
                act.wait_ge(turned, k + 1)
                at_least(act, squares_summed, k - 1)
                act.activation(squares[k % 2][0:NODE_P, :, :].rearrange("p g c -> p (g c)"), node_ps[k % 4],
                               ACT.Square).then_inc(squared, 1)

            def root(k):
                act.wait_ge(squares_summed, k + 1)
                act.activation(deviation[0:NODE_P, k], sum_sq[0:NODE_P, k], ACT.Sqrt,
                               bias=eps_col[0:NODE_P, 0:1], scale=1.0 / ROW).then_inc(rooted, 1)

            read_fold(0)
            for k in range(n_steps):
                if k + 1 < n_steps:
                    read_fold(k + 1)
                square(k)
                if k > 0:
                    root(k - 1)
            root(n_steps - 1)

        @block.vector
        def _(dve):
            dve.memset(acc[:, 0, 0:nodes_pad // 2], 0.0).then_inc(zeroed, 1)
            dve.memset(zero_row[:, :], 0.0).then_inc(zeroed, 1)
            for s in range(2):
                dve.memset(hidden[s][64:P, :], 0.0).then_inc(zeroed, 1)
            dve.wait_ge(zeroed, 4)
            for s in range(2):
                dve.memset(hidden[s][64:65, :], 1.0).then_inc(zeroed, 1)
            dve.memset(one_col[:, :], 1.0).then_inc(zeroed, 1)
            dve.memset(eps_col[:, :], EPS).then_inc(zeroed, 1)
            dve.memset(win_ps[:, :, :], 0.0).then_inc(zeroed, 1)

            dve.wait_ge(dst_in, 32)
            dve.tensor_tensor(neg_local[:, :].rearrange("p (b t) -> p b t", t=TILES),
                              first_sb[:, :].unsqueeze(2).broadcast_to([P, padded, TILES]),
                              dst_sb[:, :].rearrange("p (b t) -> p b t", t=TILES),
                              ALU.subtract).then_inc(checked, 1)
            dve.wait_ge(checked, 1)
            dve.tensor_reduce(span[:, 0:1], neg_local[:, :], AX_X, ALU.max).then_inc(checked, 1)
            dve.tensor_reduce(span[:, 1:2], neg_local[:, :], AX_X, ALU.min).then_inc(checked, 1)
            dve.wait_ge(checked, 3)
            dve.tensor_scalar(span[:, 2:3], span[:, 1:2], -1.0, float(1 - WINDOW), ALU.mult, ALU.add).then_inc(checked, 1)
            dve.wait_ge(checked, 4)
            dve.wait_ge(zeroed, 9)
            dve.tensor_tensor(span[:, 3:4], span[:, 0:1], span[:, 2:3], ALU.max).then_inc(viol_ready, 1)
            dve.wait_ge(viol_row, 1)
            dve.tensor_reduce(worst[:, 0:1], win_ps[0:1, 0, 0:P], AX_X, ALU.max).then_inc(checked, 1)
            dve.wait_ge(checked, 5)
            dve.tensor_scalar(general[:, :], worst[:, 0:1], 0.0, None, ALU.is_gt).then_inc(flag_ready, 1)
            dve.wait_ge(consts_in, 16 * 5)
            self_w = cst[SELF_ROW:SELF_ROW + ROW, C_FOLD[1]:C_FOLD[1] + ROW]
            dve.tensor_scalar(self_w, self_w, float(MUL) ** -0.5, None, ALU.mult).then_inc(checked, 1)
            both = cst[:, C_FOLD[0]:C_ALL].rearrange("p (c o) -> p c o", o=ROW)
            dve.wait_ge(checked, 6)
            dve.tensor_reduce(fold_sum[:, :], both, AX_X, ALU.add).then_inc(checked, 1)
            dve.wait_ge(checked, 7)
            dve.scalar_tensor_tensor(
                out=both, in0=fold_sum[:, :].unsqueeze(2).broadcast_to([P, 2, ROW]), scalar=-1.0 / ROW, in1=both,
                op0=ALU.mult, op1=ALU.add).then_inc(fold_centred, 1)

            def messages(i, u, n):
                g = UNROLL * i + u
                shv = sh_slot[u // LOAD][:, u % LOAD, 0:n, :]
                r, y, w, m = (a[:, 0:n] for a in (rows[:, u], inputs[u % 2], w_ps[u % 2], msg[u % 2]))
                at_least(dve, msg_ready, g)
                dve.wait_ge(gathered[u], 64 * i + 16 * n)
                if u % LOAD == 0:
                    dve.wait_ge(sh_in[u // LOAD], 16 * i + 16)
                dve.tensor_tensor(v_sh1[:, 0:n, :, :], r[:, :, 0:S_COL].rearrange("p t (m i) -> p t m i", m=3),
                                  shv[:, :, 1:4].unsqueeze(3).broadcast_to([P, n, 3, MUL]),
                                  ALU.mult).then_inc(v_sh1_done, 1)
                dve.wait_ge(w_ready, g + 1)
                dve.tensor_tensor(prod_s[:, 0:n, :, :],
                                  w[:, :, W011:W_ALL].rearrange("p t (i o) -> p t i o", o=MUL),
                                  r[:, :, S_COL:ROW].unsqueeze(3).broadcast_to([P, n, MUL, MUL]),
                                  ALU.mult).then_inc(prod_s_done, 1)
                dve.wait_ge(v_sh1_done, g + 1)
                dve.tensor_reduce(y[:, :, B_COL:B_COL + MUL], v_sh1[:, 0:n, :, :].rearrange("p t m i -> p t i m"),
                                  AX_X, ALU.add).then_inc(b_done, 1)
                dve.wait_ge(scaled, g + 1)
                dve.tensor_tensor(
                    prod[:, 0:n, 0:3, :].rearrange("p t m (i o) -> p t m i o", o=MUL),
                    w[:, :, W101:W000].rearrange("p t (i o) -> p t i o", o=MUL).unsqueeze(2)
                    .broadcast_to([P, n, 3, MUL, MUL]),
                    y[:, :, 0:S_COL].rearrange("p t (m i) -> p t m i", m=3).unsqueeze(4)
                    .broadcast_to([P, n, 3, MUL, MUL]), ALU.mult).then_inc(prod_v_done, 1)
                dve.wait_ge(b_done, g + 1)
                dve.tensor_tensor(
                    prod[:, 0:n, 3:5, :].rearrange("p t b (i o) -> p t (b i) o", o=MUL),
                    w[:, :, W000:W011].rearrange("p t (i o) -> p t i o", o=MUL),
                    y[:, :, S_COL:ROW + MUL].unsqueeze(3).broadcast_to([P, n, 2 * MUL, MUL]),
                    ALU.mult).then_inc(prods_done, 1)
                dve.wait_ge(prod_s_done, g + 1)
                dve.tensor_reduce(sum_s[:, 0:n, :], prod_s[:, 0:n, :, :].rearrange("p t i o -> p t o i"),
                                  AX_X, ALU.add).then_inc(sum_s_done, 1)
                dve.wait_ge(prod_v_done, g + 1)
                dve.wait_ge(prods_done, g + 1)
                at_least(dve, scattered, g - 1)
                dve.tensor_tensor(m[:, :, 0:T_COL].rearrange("p t (b c) -> p t b c", c=HALF),
                                  prod[:, 0:n, :, 0:HALF], prod[:, 0:n, :, HALF:2 * HALF],
                                  ALU.add)
                dve.wait_ge(sum_s_done, g + 1)
                dve.tensor_tensor(m[:, :, T_COL:MSG].rearrange("p t (m o) -> p t m o", m=3),
                                  sum_s[:, 0:n, :].unsqueeze(2).broadcast_to([P, n, 3, MUL]),
                                  shv[:, :, 1:4].unsqueeze(3).broadcast_to([P, n, 3, MUL]),
                                  ALU.mult).then_inc(msg_ready, 1)

            def accumulate(i, u, n, slow):
                g = UNROLL * i + u
                if slow:
                    done = g + 1 if isinstance(g, int) else dve.snap(g + 1)
                    dve.wait_ge(flag_ready, 1)
                    dve.wait_ge(scattered, done)
                    for t in range(n):
                        col = (t % 2) * 256
                        with dve.Fori(0, P) as e:
                            node = dve.value_load(dst_rows[:, bass.ds(g * BATCH + t * P + e, 1)],
                                                  min_val=0, max_val=n_nodes - 1)
                            to = acc[:, :, bass.ds(node, 1)]
                            column = win_ps[:, t // 2, bass.ds(e + col, P + 1)][:, 0:P + 1:P].unsqueeze(2)
                            dve.tensor_tensor(to, to, column, ALU.add)
                            dve.drain()
                    dve.sem_inc(acc_done, 1)
                    return
                node = dve.value_load(first_sb[0:1, bass.ds(g, 1)], min_val=0, max_val=n_nodes - 1)
                at_least(dve, acc_done, g)
                dve.wait_ge(scattered, g + 1)
                to = acc[:, :, bass.ds(node, WINDOW)]
                dve.tensor_tensor(to, to, win_ps[:, u % 2, 0:2 * WINDOW].rearrange("p (c n) -> p c n", c=2),
                                  ALU.add).then_inc(acc_done, 1)

            def edges(slow):
                dve.wait_ge(acc_zeroed, 1)
                dve.wait_ge(acc_copied, 16)
                dve.wait_ge(x_in, 32)

                def step(i, first, last):
                    for u in range(batches(last)):
                        messages(i, u, tiles(u, last))
                        if not first or u > 0:
                            accumulate(i, u - 1, TILES, slow)

                iterations(dve, step)
                accumulate(n_iters - 1, tail - 1, tail_tiles, slow)

            dve.wait_ge(flag_ready, 1)
            flag = dve.value_load(general[0:1, 0:1], min_val=0, max_val=1)
            with dve.If(flag == 0):
                edges(False)
            with dve.Else():
                edges(True)

            def sum_squares(k):
                dve.wait_ge(squared, k + 1)
                dve.tensor_reduce(sum_sq[0:NODE_P, k, :], squares[k % 2][0:NODE_P, :, :], AX_X,
                                  ALU.add).then_inc(squares_summed, 1)

            def normalise(k):
                dve.wait_ge(rooted, k + 1)
                dve.reciprocal(inverse[0:NODE_P, k], deviation[0:NODE_P, k]).then_inc(inverted, 1)
                dve.wait_ge(inverted, k + 1)
                dve.tensor_tensor(
                    y_sb[0:NODE_P, k, :, :].rearrange("p q (j c) -> p j q c", j=NODE_J),
                    node_ps[k % 4].rearrange("p (j q c) -> p j q c", j=NODE_J, q=QUARTERS),
                    inverse[0:NODE_P, k, :].rearrange("p (j q) -> p j q", j=NODE_J).unsqueeze(3)
                    .broadcast_to([NODE_P, NODE_J, QUARTERS, ROW]), ALU.mult).then_inc(y_ready, 1)

            for k in range(n_steps):
                sum_squares(k)
                if k > 0:
                    normalise(k - 1)
            normalise(n_steps - 1)


def constants():
    import numpy as np

    c = np.zeros((P, C_ALL), np.float32)
    c[:, C_EYE:C_EYE + P] = np.eye(P, dtype=np.float32)
    c[:, C_IOTA:C_IOTA + WINDOW] = np.arange(WINDOW, dtype=np.float32)
    c110 = 1.0 / np.sqrt(3.0)
    for o in range(MUL):
        for part in range(MUL // 2):
            for m in range(3):
                c[m * HALF + part * MUL + o, C_FOLD[0] + MUL + 3 * o + m] = ALPHA
            c[3 * HALF + part * MUL + o, C_FOLD[0] + o] = ALPHA
            c[part * MUL + o, C_FOLD[1] + o] = ALPHA * c110
        for m in range(3):
            c[HALF + m * MUL + o, C_FOLD[1] + MUL + 3 * o + m] = ALPHA
            c[SELF_ROW + ROW + m * MUL + o, C_FOLD[1] + MUL + 3 * o + m] = 1.0
        c[SELF_ROW + ROW + S_COL + o, C_FOLD[1] + o] = 1.0
    return c


def layouts(x, src, dst, edge_attr_32, edge_attr_4, L0_gnn_W1, L0_gnn_b1, L0_gnn_W2, L0_gnn_b2,
            L0_gnn_si_w0, L0_gnn_si_w1):
    import numpy as np

    x, src, dst, feat, sh = (np.asarray(a) for a in (x, src, dst, edge_attr_32, edge_attr_4))
    n, e = x.shape[0], src.shape[0]
    batches = -(-e // (LOAD * BATCH)) * LOAD
    pad = batches * BATCH - e
    steps = -(-(n + WINDOW) // (QUARTERS * NODE_STEP))
    src = np.pad(src, (0, pad), mode="edge")
    dst = np.pad(dst, (0, pad), mode="edge")
    feat = np.pad(feat, ((0, pad), (0, 0)))
    sh = np.pad(sh, ((0, pad), (0, 0)))
    x_rows = np.concatenate([x[:, 8:].reshape(n, 8, 3).transpose(0, 2, 1).reshape(n, 24), x[:, :8]], axis=1)
    more = steps * QUARTERS * NODE_STEP - n
    w2 = np.asarray(L0_gnn_W2).reshape(64, 4, 64)[:, [2, 0, 3, 1]].reshape(64, 256)
    b2 = np.asarray(L0_gnn_b2).reshape(1, 4, 64)[:, [2, 0, 3, 1]].reshape(1, 256)
    w1 = np.zeros((TILES, 32, TILES, 64), x.dtype)
    for t in range(TILES):
        w1[t, :, t] = np.asarray(L0_gnn_W1)
    w2 = np.pad(np.concatenate([w2, b2]), ((0, P - 65), (0, 0)))
    consts = constants()
    fold_b = consts[:, C_FOLD[1]:].copy()
    self_w = fold_b[SELF_ROW:SELF_ROW + ROW]
    self_w[24:, :8] = np.asarray(L0_gnn_si_w0)
    for m in range(3):
        self_w[8 * m:8 * m + 8, 8 + m::3] = np.asarray(L0_gnn_si_w1)
    return {
        "x_rows": x_rows,
        "x_cols": np.pad(x_rows, ((0, more), (0, 0))).T,
        "src": src.reshape(batches * TILES, P).T,
        "dst": dst.reshape(batches * TILES, P).T,
        "dst_first": dst[::BATCH].reshape(1, batches),
        "dst_rows": dst.reshape(1, -1),
        "feat": feat.reshape(batches, TILES, P, 32).transpose(1, 3, 0, 2).reshape(P, -1),
        "sh": sh.reshape(batches * TILES, P, 4).transpose(1, 0, 2).reshape(P, -1),
        "w1": w1.reshape(P, -1),
        "b1": np.tile(np.asarray(L0_gnn_b1), 2).reshape(P, 1),
        "w2": w2,
        "self_in_w": fold_b,
        "consts": consts,
    }


def kernel(**inputs):
    import numpy as np
    import concourse.bacc as bacc
    from concourse.bass_utils import run_bass_kernel_spmd

    nc = bacc.Bacc("TRN2", target_bir_lowering=False, num_devices=1)
    arrays = {k: np.ascontiguousarray(a) for k, a in layouts(**inputs).items()}
    args = {k: nc.dram_tensor(f"{k}_dram", a.shape, mybir.dt.from_np(a.dtype), kind="ExternalInput").ap()
            for k, a in arrays.items()}
    out = nc.dram_tensor("out_dram", inputs["x"].shape, F32, kind="ExternalOutput").ap()
    build(nc, out=out, n_tiles=-(-inputs["src"].shape[0] // P), **args)
    r = run_bass_kernel_spmd(nc, [{f"{k}_dram": a for k, a in arrays.items()}], core_ids=[0])
    return r.results[0]["out_dram"]
```
